# Optimizing a Trainium2 kernel written in Bass

```python
import numpy as np
import jax
import jax.numpy as jnp

def _softmax(x, axis=-1):
    return jax.nn.softmax(x, axis=axis)

def _gelu(x):
    return jax.nn.gelu(x, approximate=True)

def _silu(x):
    return jax.nn.silu(x)

def _sigmoid(x):
    return jax.nn.sigmoid(x)

def _layernorm(x, axis=-1, eps=1e-05):
    m = jnp.mean(x, axis=axis, keepdims=True)
    v = jnp.var(x, axis=axis, keepdims=True)
    return (x - m) / jnp.sqrt(v + eps)

def _scatter_add(tgt, idx, src, axis=0):
    return tgt.at[idx].add(src)

def _segment_sum(src, seg, n):
    return jax.ops.segment_sum(src, seg, n)
kernel_name = 'mk_rec_standalone_d1_rec_r8_85f9b7'

def setup_inputs(seed: int=0):
    np.random.seed(seed)
    _w = jnp.asarray

    def _rec_inputs():
        import jax
        import jax.numpy as jnp
        _rk = jax.random.key(seed)
        r_sequence_ids = jnp.stack([jax.random.randint(jax.random.fold_in(jax.random.fold_in(_rk, 1), 0), (2048,), 5, 99326, jnp.int32), jax.random.randint(jax.random.fold_in(jax.random.fold_in(_rk, 1), 1), (2048,), 220, 99995, jnp.int32), jax.random.randint(jax.random.fold_in(jax.random.fold_in(_rk, 1), 2), (2048,), 265, 99940, jnp.int32), jax.random.randint(jax.random.fold_in(jax.random.fold_in(_rk, 1), 3), (2048,), 402, 99940, jnp.int32), jax.random.randint(jax.random.fold_in(jax.random.fold_in(_rk, 1), 4), (2048,), 225, 99931, jnp.int32), jax.random.randint(jax.random.fold_in(jax.random.fold_in(_rk, 1), 5), (2048,), 106, 12497, jnp.int32), jax.random.randint(jax.random.fold_in(jax.random.fold_in(_rk, 1), 6), (2048,), 132, 99942, jnp.int32), jax.random.randint(jax.random.fold_in(jax.random.fold_in(_rk, 1), 7), (2048,), 167, 12486, jnp.int32), jax.random.randint(jax.random.fold_in(jax.random.fold_in(_rk, 1), 8), (2048,), 58, 99725, jnp.int32), jax.random.randint(jax.random.fold_in(jax.random.fold_in(_rk, 1), 9), (2048,), 63, 99973, jnp.int32), jax.random.randint(jax.random.fold_in(jax.random.fold_in(_rk, 1), 10), (2048,), 38, 99849, jnp.int32), jax.random.randint(jax.random.fold_in(jax.random.fold_in(_rk, 1), 11), (2048,), 123, 99892, jnp.int32), jax.random.randint(jax.random.fold_in(jax.random.fold_in(_rk, 1), 12), (2048,), 56, 99898, jnp.int32), jax.random.randint(jax.random.fold_in(jax.random.fold_in(_rk, 1), 13), (2048,), 37, 99812, jnp.int32), jax.random.randint(jax.random.fold_in(jax.random.fold_in(_rk, 1), 14), (2048,), 27, 12482, jnp.int32), jax.random.randint(jax.random.fold_in(jax.random.fold_in(_rk, 1), 15), (2048,), 0, 99865, jnp.int32), jax.random.randint(jax.random.fold_in(jax.random.fold_in(_rk, 1), 16), (2048,), 56, 99762, jnp.int32), jax.random.randint(jax.random.fold_in(jax.random.fold_in(_rk, 1), 17), (2048,), 405, 99982, jnp.int32), jax.random.randint(jax.random.fold_in(jax.random.fold_in(_rk, 1), 18), (2048,), 30, 99955, jnp.int32), jax.random.randint(jax.random.fold_in(jax.random.fold_in(_rk, 1), 19), (2048,), 40, 99908, jnp.int32), jax.random.randint(jax.random.fold_in(jax.random.fold_in(_rk, 1), 20), (2048,), 58, 12490, jnp.int32), jax.random.randint(jax.random.fold_in(jax.random.fold_in(_rk, 1), 21), (2048,), 5, 99876, jnp.int32), jax.random.randint(jax.random.fold_in(jax.random.fold_in(_rk, 1), 22), (2048,), 117, 99957, jnp.int32), jax.random.randint(jax.random.fold_in(jax.random.fold_in(_rk, 1), 23), (2048,), 172, 99956, jnp.int32), jax.random.randint(jax.random.fold_in(jax.random.fold_in(_rk, 1), 24), (2048,), 331, 99903, jnp.int32), jax.random.randint(jax.random.fold_in(jax.random.fold_in(_rk, 1), 25), (2048,), 10, 99683, jnp.int32), jax.random.randint(jax.random.fold_in(jax.random.fold_in(_rk, 1), 26), (2048,), 38, 99669, jnp.int32), jax.random.randint(jax.random.fold_in(jax.random.fold_in(_rk, 1), 27), (2048,), 376, 99905, jnp.int32), jax.random.randint(jax.random.fold_in(jax.random.fold_in(_rk, 1), 28), (2048,), 105, 12487, jnp.int32), jax.random.randint(jax.random.fold_in(jax.random.fold_in(_rk, 1), 29), (2048,), 39, 99994, jnp.int32), jax.random.randint(jax.random.fold_in(jax.random.fold_in(_rk, 1), 30), (2048,), 38, 99982, jnp.int32), jax.random.randint(jax.random.fold_in(jax.random.fold_in(_rk, 1), 31), (2048,), 3, 99946, jnp.int32), jax.random.randint(jax.random.fold_in(jax.random.fold_in(_rk, 1), 32), (2048,), 79, 99983, jnp.int32), jax.random.randint(jax.random.fold_in(jax.random.fold_in(_rk, 1), 33), (2048,), 7, 99947, jnp.int32), jax.random.randint(jax.random.fold_in(jax.random.fold_in(_rk, 1), 34), (2048,), 67, 99937, jnp.int32), jax.random.randint(jax.random.fold_in(jax.random.fold_in(_rk, 1), 35), (2048,), 90, 99989, jnp.int32), jax.random.randint(jax.random.fold_in(jax.random.fold_in(_rk, 1), 36), (2048,), 6, 99980, jnp.int32), jax.random.randint(jax.random.fold_in(jax.random.fold_in(_rk, 1), 37), (2048,), 71, 99917, jnp.int32), jax.random.randint(jax.random.fold_in(jax.random.fold_in(_rk, 1), 38), (2048,), 44, 99770, jnp.int32), jax.random.randint(jax.random.fold_in(jax.random.fold_in(_rk, 1), 39), (2048,), 23, 99988, jnp.int32), jax.random.randint(jax.random.fold_in(jax.random.fold_in(_rk, 1), 40), (2048,), 48, 99913, jnp.int32), jax.random.randint(jax.random.fold_in(jax.random.fold_in(_rk, 1), 41), (2048,), 45, 99942, jnp.int32), jax.random.randint(jax.random.fold_in(jax.random.fold_in(_rk, 1), 42), (2048,), 130, 99942, jnp.int32), jax.random.randint(jax.random.fold_in(jax.random.fold_in(_rk, 1), 43), (2048,), 26, 99979, jnp.int32), jax.random.randint(jax.random.fold_in(jax.random.fold_in(_rk, 1), 44), (2048,), 62, 99914, jnp.int32), jax.random.randint(jax.random.fold_in(jax.random.fold_in(_rk, 1), 45), (2048,), 246, 12498, jnp.int32), jax.random.randint(jax.random.fold_in(jax.random.fold_in(_rk, 1), 46), (2048,), 139, 99810, jnp.int32), jax.random.randint(jax.random.fold_in(jax.random.fold_in(_rk, 1), 47), (2048,), 129, 99751, jnp.int32), jax.random.randint(jax.random.fold_in(jax.random.fold_in(_rk, 1), 48), (2048,), 176, 99915, jnp.int32), jax.random.randint(jax.random.fold_in(jax.random.fold_in(_rk, 1), 49), (2048,), 111, 99945, jnp.int32), jax.random.randint(jax.random.fold_in(jax.random.fold_in(_rk, 1), 50), (2048,), 224, 99916, jnp.int32), jax.random.randint(jax.random.fold_in(jax.random.fold_in(_rk, 1), 51), (2048,), 89, 99895, jnp.int32), jax.random.randint(jax.random.fold_in(jax.random.fold_in(_rk, 1), 52), (2048,), 347, 99926, jnp.int32), jax.random.randint(jax.random.fold_in(jax.random.fold_in(_rk, 1), 53), (2048,), 33, 99963, jnp.int32), jax.random.randint(jax.random.fold_in(jax.random.fold_in(_rk, 1), 54), (2048,), 9, 99964, jnp.int32), jax.random.randint(jax.random.fold_in(jax.random.fold_in(_rk, 1), 55), (2048,), 61, 99812, jnp.int32), jax.random.randint(jax.random.fold_in(jax.random.fold_in(_rk, 1), 56), (2048,), 88, 99907, jnp.int32), jax.random.randint(jax.random.fold_in(jax.random.fold_in(_rk, 1), 57), (2048,), 84, 99981, jnp.int32), jax.random.randint(jax.random.fold_in(jax.random.fold_in(_rk, 1), 58), (2048,), 356, 99987, jnp.int32), jax.random.randint(jax.random.fold_in(jax.random.fold_in(_rk, 1), 59), (2048,), 14, 99914, jnp.int32), jax.random.randint(jax.random.fold_in(jax.random.fold_in(_rk, 1), 60), (2048,), 24, 99983, jnp.int32), jax.random.randint(jax.random.fold_in(jax.random.fold_in(_rk, 1), 61), (2048,), 63, 99972, jnp.int32), jax.random.randint(jax.random.fold_in(jax.random.fold_in(_rk, 1), 62), (2048,), 257, 99965, jnp.int32), jax.random.randint(jax.random.fold_in(jax.random.fold_in(_rk, 1), 63), (2048,), 14, 99926, jnp.int32), jax.random.randint(jax.random.fold_in(jax.random.fold_in(_rk, 1), 64), (2048,), 200, 99972, jnp.int32), jax.random.randint(jax.random.fold_in(jax.random.fold_in(_rk, 1), 65), (2048,), 176, 99982, jnp.int32), jax.random.randint(jax.random.fold_in(jax.random.fold_in(_rk, 1), 66), (2048,), 26, 99995, jnp.int32), jax.random.randint(jax.random.fold_in(jax.random.fold_in(_rk, 1), 67), (2048,), 41, 99929, jnp.int32), jax.random.randint(jax.random.fold_in(jax.random.fold_in(_rk, 1), 68), (2048,), 17, 99966, jnp.int32), jax.random.randint(jax.random.fold_in(jax.random.fold_in(_rk, 1), 69), (2048,), 60, 99726, jnp.int32), jax.random.randint(jax.random.fold_in(jax.random.fold_in(_rk, 1), 70), (2048,), 15, 99564, jnp.int32), jax.random.randint(jax.random.fold_in(jax.random.fold_in(_rk, 1), 71), (2048,), 21, 99913, jnp.int32), jax.random.randint(jax.random.fold_in(jax.random.fold_in(_rk, 1), 72), (2048,), 82, 12496, jnp.int32), jax.random.randint(jax.random.fold_in(jax.random.fold_in(_rk, 1), 73), (2048,), 161, 99945, jnp.int32), jax.random.randint(jax.random.fold_in(jax.random.fold_in(_rk, 1), 74), (2048,), 180, 99761, jnp.int32), jax.random.randint(jax.random.fold_in(jax.random.fold_in(_rk, 1), 75), (2048,), 78, 99910, jnp.int32), jax.random.randint(jax.random.fold_in(jax.random.fold_in(_rk, 1), 76), (2048,), 34, 99999, jnp.int32), jax.random.randint(jax.random.fold_in(jax.random.fold_in(_rk, 1), 77), (2048,), 15, 99962, jnp.int32), jax.random.randint(jax.random.fold_in(jax.random.fold_in(_rk, 1), 78), (2048,), 142, 99878, jnp.int32), jax.random.randint(jax.random.fold_in(jax.random.fold_in(_rk, 1), 79), (2048,), 127, 99921, jnp.int32), jax.random.randint(jax.random.fold_in(jax.random.fold_in(_rk, 1), 80), (2048,), 41, 12487, jnp.int32), jax.random.randint(jax.random.fold_in(jax.random.fold_in(_rk, 1), 81), (2048,), 121, 99940, jnp.int32), jax.random.randint(jax.random.fold_in(jax.random.fold_in(_rk, 1), 82), (2048,), 10, 99969, jnp.int32), jax.random.randint(jax.random.fold_in(jax.random.fold_in(_rk, 1), 83), (2048,), 93, 99985, jnp.int32), jax.random.randint(jax.random.fold_in(jax.random.fold_in(_rk, 1), 84), (2048,), 54, 12481, jnp.int32), jax.random.randint(jax.random.fold_in(jax.random.fold_in(_rk, 1), 85), (2048,), 2, 99973, jnp.int32), jax.random.randint(jax.random.fold_in(jax.random.fold_in(_rk, 1), 86), (2048,), 1, 99947, jnp.int32), jax.random.randint(jax.random.fold_in(jax.random.fold_in(_rk, 1), 87), (2048,), 12, 99695, jnp.int32), jax.random.randint(jax.random.fold_in(jax.random.fold_in(_rk, 1), 88), (2048,), 136, 99797, jnp.int32), jax.random.randint(jax.random.fold_in(jax.random.fold_in(_rk, 1), 89), (2048,), 219, 99866, jnp.int32), jax.random.randint(jax.random.fold_in(jax.random.fold_in(_rk, 1), 90), (2048,), 6, 99770, jnp.int32), jax.random.randint(jax.random.fold_in(jax.random.fold_in(_rk, 1), 91), (2048,), 100, 99969, jnp.int32), jax.random.randint(jax.random.fold_in(jax.random.fold_in(_rk, 1), 92), (2048,), 126, 99962, jnp.int32), jax.random.randint(jax.random.fold_in(jax.random.fold_in(_rk, 1), 93), (2048,), 29, 99777, jnp.int32), jax.random.randint(jax.random.fold_in(jax.random.fold_in(_rk, 1), 94), (2048,), 50, 99921, jnp.int32), jax.random.randint(jax.random.fold_in(jax.random.fold_in(_rk, 1), 95), (2048,), 141, 99959, jnp.int32), jax.random.randint(jax.random.fold_in(jax.random.fold_in(_rk, 1), 96), (2048,), 0, 99970, jnp.int32), jax.random.randint(jax.random.fold_in(jax.random.fold_in(_rk, 1), 97), (2048,), 76, 99749, jnp.int32), jax.random.randint(jax.random.fold_in(jax.random.fold_in(_rk, 1), 98), (2048,), 130, 99981, jnp.int32), jax.random.randint(jax.random.fold_in(jax.random.fold_in(_rk, 1), 99), (2048,), 334, 12488, jnp.int32), jax.random.randint(jax.random.fold_in(jax.random.fold_in(_rk, 1), 100), (2048,), 230, 99892, jnp.int32), jax.random.randint(jax.random.fold_in(jax.random.fold_in(_rk, 1), 101), (2048,), 118, 99963, jnp.int32), jax.random.randint(jax.random.fold_in(jax.random.fold_in(_rk, 1), 102), (2048,), 144, 99875, jnp.int32), jax.random.randint(jax.random.fold_in(jax.random.fold_in(_rk, 1), 103), (2048,), 134, 99943, jnp.int32), jax.random.randint(jax.random.fold_in(jax.random.fold_in(_rk, 1), 104), (2048,), 28, 99963, jnp.int32), jax.random.randint(jax.random.fold_in(jax.random.fold_in(_rk, 1), 105), (2048,), 2, 99743, jnp.int32), jax.random.randint(jax.random.fold_in(jax.random.fold_in(_rk, 1), 106), (2048,), 43, 12496, jnp.int32), jax.random.randint(jax.random.fold_in(jax.random.fold_in(_rk, 1), 107), (2048,), 10, 99919, jnp.int32), jax.random.randint(jax.random.fold_in(jax.random.fold_in(_rk, 1), 108), (2048,), 100, 99874, jnp.int32), jax.random.randint(jax.random.fold_in(jax.random.fold_in(_rk, 1), 109), (2048,), 227, 99951, jnp.int32), jax.random.randint(jax.random.fold_in(jax.random.fold_in(_rk, 1), 110), (2048,), 3, 99893, jnp.int32), jax.random.randint(jax.random.fold_in(jax.random.fold_in(_rk, 1), 111), (2048,), 10, 99999, jnp.int32), jax.random.randint(jax.random.fold_in(jax.random.fold_in(_rk, 1), 112), (2048,), 96, 99961, jnp.int32), jax.random.randint(jax.random.fold_in(jax.random.fold_in(_rk, 1), 113), (2048,), 31, 99951, jnp.int32), jax.random.randint(jax.random.fold_in(jax.random.fold_in(_rk, 1), 114), (2048,), 271, 99734, jnp.int32), jax.random.randint(jax.random.fold_in(jax.random.fold_in(_rk, 1), 115), (2048,), 14, 99881, jnp.int32), jax.random.randint(jax.random.fold_in(jax.random.fold_in(_rk, 1), 116), (2048,), 57, 99982, jnp.int32), jax.random.randint(jax.random.fold_in(jax.random.fold_in(_rk, 1), 117), (2048,), 49, 12497, jnp.int32), jax.random.randint(jax.random.fold_in(jax.random.fold_in(_rk, 1), 118), (2048,), 6, 99995, jnp.int32), jax.random.randint(jax.random.fold_in(jax.random.fold_in(_rk, 1), 119), (2048,), 65, 99870, jnp.int32), jax.random.randint(jax.random.fold_in(jax.random.fold_in(_rk, 1), 120), (2048,), 29, 12495, jnp.int32), jax.random.randint(jax.random.fold_in(jax.random.fold_in(_rk, 1), 121), (2048,), 9, 99951, jnp.int32), jax.random.randint(jax.random.fold_in(jax.random.fold_in(_rk, 1), 122), (2048,), 47, 99740, jnp.int32), jax.random.randint(jax.random.fold_in(jax.random.fold_in(_rk, 1), 123), (2048,), 23, 99898, jnp.int32), jax.random.randint(jax.random.fold_in(jax.random.fold_in(_rk, 1), 124), (2048,), 97, 99947, jnp.int32), jax.random.randint(jax.random.fold_in(jax.random.fold_in(_rk, 1), 125), (2048,), 278, 99926, jnp.int32), jax.random.randint(jax.random.fold_in(jax.random.fold_in(_rk, 1), 126), (2048,), 64, 12475, jnp.int32), jax.random.randint(jax.random.fold_in(jax.random.fold_in(_rk, 1), 127), (2048,), 51, 99692, jnp.int32), jax.random.randint(jax.random.fold_in(jax.random.fold_in(_rk, 1), 128), (2048,), 89, 99898, jnp.int32), jax.random.randint(jax.random.fold_in(jax.random.fold_in(_rk, 1), 129), (2048,), 91, 99924, jnp.int32), jax.random.randint(jax.random.fold_in(jax.random.fold_in(_rk, 1), 130), (2048,), 140, 99787, jnp.int32), jax.random.randint(jax.random.fold_in(jax.random.fold_in(_rk, 1), 131), (2048,), 243, 99902, jnp.int32), jax.random.randint(jax.random.fold_in(jax.random.fold_in(_rk, 1), 132), (2048,), 15, 99925, jnp.int32), jax.random.randint(jax.random.fold_in(jax.random.fold_in(_rk, 1), 133), (2048,), 64, 12479, jnp.int32), jax.random.randint(jax.random.fold_in(jax.random.fold_in(_rk, 1), 134), (2048,), 68, 99897, jnp.int32), jax.random.randint(jax.random.fold_in(jax.random.fold_in(_rk, 1), 135), (2048,), 48, 99724, jnp.int32), jax.random.randint(jax.random.fold_in(jax.random.fold_in(_rk, 1), 136), (2048,), 69, 99654, jnp.int32), jax.random.randint(jax.random.fold_in(jax.random.fold_in(_rk, 1), 137), (2048,), 13, 99799, jnp.int32), jax.random.randint(jax.random.fold_in(jax.random.fold_in(_rk, 1), 138), (2048,), 37, 12499, jnp.int32), jax.random.randint(jax.random.fold_in(jax.random.fold_in(_rk, 1), 139), (2048,), 77, 99868, jnp.int32), jax.random.randint(jax.random.fold_in(jax.random.fold_in(_rk, 1), 140), (2048,), 16, 12496, jnp.int32), jax.random.randint(jax.random.fold_in(jax.random.fold_in(_rk, 1), 141), (2048,), 433, 99942, jnp.int32), jax.random.randint(jax.random.fold_in(jax.random.fold_in(_rk, 1), 142), (2048,), 37, 99875, jnp.int32), jax.random.randint(jax.random.fold_in(jax.random.fold_in(_rk, 1), 143), (2048,), 18, 99975, jnp.int32), jax.random.randint(jax.random.fold_in(jax.random.fold_in(_rk, 1), 144), (2048,), 54, 99906, jnp.int32), jax.random.randint(jax.random.fold_in(jax.random.fold_in(_rk, 1), 145), (2048,), 19, 99981, jnp.int32), jax.random.randint(jax.random.fold_in(jax.random.fold_in(_rk, 1), 146), (2048,), 67, 99994, jnp.int32), jax.random.randint(jax.random.fold_in(jax.random.fold_in(_rk, 1), 147), (2048,), 88, 99953, jnp.int32), jax.random.randint(jax.random.fold_in(jax.random.fold_in(_rk, 1), 148), (2048,), 14, 99946, jnp.int32), jax.random.randint(jax.random.fold_in(jax.random.fold_in(_rk, 1), 149), (2048,), 161, 99876, jnp.int32), jax.random.randint(jax.random.fold_in(jax.random.fold_in(_rk, 1), 150), (2048,), 106, 99987, jnp.int32), jax.random.randint(jax.random.fold_in(jax.random.fold_in(_rk, 1), 151), (2048,), 57, 12486, jnp.int32), jax.random.randint(jax.random.fold_in(jax.random.fold_in(_rk, 1), 152), (2048,), 2, 12496, jnp.int32), jax.random.randint(jax.random.fold_in(jax.random.fold_in(_rk, 1), 153), (2048,), 77, 12477, jnp.int32), jax.random.randint(jax.random.fold_in(jax.random.fold_in(_rk, 1), 154), (2048,), 2, 99578, jnp.int32), jax.random.randint(jax.random.fold_in(jax.random.fold_in(_rk, 1), 155), (2048,), 96, 99969, jnp.int32), jax.random.randint(jax.random.fold_in(jax.random.fold_in(_rk, 1), 156), (2048,), 114, 99932, jnp.int32), jax.random.randint(jax.random.fold_in(jax.random.fold_in(_rk, 1), 157), (2048,), 9, 99751, jnp.int32), jax.random.randint(jax.random.fold_in(jax.random.fold_in(_rk, 1), 158), (2048,), 92, 99909, jnp.int32), jax.random.randint(jax.random.fold_in(jax.random.fold_in(_rk, 1), 159), (2048,), 10, 12475, jnp.int32), jax.random.randint(jax.random.fold_in(jax.random.fold_in(_rk, 1), 160), (2048,), 48, 99893, jnp.int32), jax.random.randint(jax.random.fold_in(jax.random.fold_in(_rk, 1), 161), (2048,), 57, 99937, jnp.int32), jax.random.randint(jax.random.fold_in(jax.random.fold_in(_rk, 1), 162), (2048,), 15, 99971, jnp.int32), jax.random.randint(jax.random.fold_in(jax.random.fold_in(_rk, 1), 163), (2048,), 27, 12497, jnp.int32), jax.random.randint(jax.random.fold_in(jax.random.fold_in(_rk, 1), 164), (2048,), 226, 99679, jnp.int32), jax.random.randint(jax.random.fold_in(jax.random.fold_in(_rk, 1), 165), (2048,), 249, 99902, jnp.int32), jax.random.randint(jax.random.fold_in(jax.random.fold_in(_rk, 1), 166), (2048,), 122, 99587, jnp.int32), jax.random.randint(jax.random.fold_in(jax.random.fold_in(_rk, 1), 167), (2048,), 511, 99853, jnp.int32), jax.random.randint(jax.random.fold_in(jax.random.fold_in(_rk, 1), 168), (2048,), 207, 99990, jnp.int32), jax.random.randint(jax.random.fold_in(jax.random.fold_in(_rk, 1), 169), (2048,), 65, 99893, jnp.int32), jax.random.randint(jax.random.fold_in(jax.random.fold_in(_rk, 1), 170), (2048,), 127, 99983, jnp.int32), jax.random.randint(jax.random.fold_in(jax.random.fold_in(_rk, 1), 171), (2048,), 10, 99942, jnp.int32), jax.random.randint(jax.random.fold_in(jax.random.fold_in(_rk, 1), 172), (2048,), 14, 99970, jnp.int32), jax.random.randint(jax.random.fold_in(jax.random.fold_in(_rk, 1), 173), (2048,), 97, 99844, jnp.int32), jax.random.randint(jax.random.fold_in(jax.random.fold_in(_rk, 1), 174), (2048,), 211, 99849, jnp.int32), jax.random.randint(jax.random.fold_in(jax.random.fold_in(_rk, 1), 175), (2048,), 111, 12498, jnp.int32), jax.random.randint(jax.random.fold_in(jax.random.fold_in(_rk, 1), 176), (2048,), 141, 99770, jnp.int32), jax.random.randint(jax.random.fold_in(jax.random.fold_in(_rk, 1), 177), (2048,), 32, 99996, jnp.int32), jax.random.randint(jax.random.fold_in(jax.random.fold_in(_rk, 1), 178), (2048,), 74, 99854, jnp.int32), jax.random.randint(jax.random.fold_in(jax.random.fold_in(_rk, 1), 179), (2048,), 27, 12498, jnp.int32), jax.random.randint(jax.random.fold_in(jax.random.fold_in(_rk, 1), 180), (2048,), 91, 99981, jnp.int32), jax.random.randint(jax.random.fold_in(jax.random.fold_in(_rk, 1), 181), (2048,), 141, 99917, jnp.int32), jax.random.randint(jax.random.fold_in(jax.random.fold_in(_rk, 1), 182), (2048,), 40, 12493, jnp.int32), jax.random.randint(jax.random.fold_in(jax.random.fold_in(_rk, 1), 183), (2048,), 31, 99867, jnp.int32), jax.random.randint(jax.random.fold_in(jax.random.fold_in(_rk, 1), 184), (2048,), 122, 99973, jnp.int32), jax.random.randint(jax.random.fold_in(jax.random.fold_in(_rk, 1), 185), (2048,), 149, 99734, jnp.int32), jax.random.randint(jax.random.fold_in(jax.random.fold_in(_rk, 1), 186), (2048,), 222, 99979, jnp.int32), jax.random.randint(jax.random.fold_in(jax.random.fold_in(_rk, 1), 187), (2048,), 69, 99964, jnp.int32), jax.random.randint(jax.random.fold_in(jax.random.fold_in(_rk, 1), 188), (2048,), 72, 99999, jnp.int32), jax.random.randint(jax.random.fold_in(jax.random.fold_in(_rk, 1), 189), (2048,), 237, 99955, jnp.int32), jax.random.randint(jax.random.fold_in(jax.random.fold_in(_rk, 1), 190), (2048,), 1, 12492, jnp.int32), jax.random.randint(jax.random.fold_in(jax.random.fold_in(_rk, 1), 191), (2048,), 42, 12472, jnp.int32), jax.random.randint(jax.random.fold_in(jax.random.fold_in(_rk, 1), 192), (2048,), 64, 99997, jnp.int32), jax.random.randint(jax.random.fold_in(jax.random.fold_in(_rk, 1), 193), (2048,), 36, 12483, jnp.int32), jax.random.randint(jax.random.fold_in(jax.random.fold_in(_rk, 1), 194), (2048,), 55, 99933, jnp.int32), jax.random.randint(jax.random.fold_in(jax.random.fold_in(_rk, 1), 195), (2048,), 122, 99868, jnp.int32), jax.random.randint(jax.random.fold_in(jax.random.fold_in(_rk, 1), 196), (2048,), 119, 99961, jnp.int32), jax.random.randint(jax.random.fold_in(jax.random.fold_in(_rk, 1), 197), (2048,), 152, 99937, jnp.int32), jax.random.randint(jax.random.fold_in(jax.random.fold_in(_rk, 1), 198), (2048,), 20, 99759, jnp.int32), jax.random.randint(jax.random.fold_in(jax.random.fold_in(_rk, 1), 199), (2048,), 27, 99851, jnp.int32)], axis=1)
        r_retrieved_indices = jnp.stack([jax.random.randint(jax.random.fold_in(jax.random.fold_in(_rk, 2), 0), (2048,), 55, 99965, jnp.int32), jax.random.randint(jax.random.fold_in(jax.random.fold_in(_rk, 2), 1), (2048,), 48, 12493, jnp.int32), jax.random.randint(jax.random.fold_in(jax.random.fold_in(_rk, 2), 2), (2048,), 149, 99818, jnp.int32), jax.random.randint(jax.random.fold_in(jax.random.fold_in(_rk, 2), 3), (2048,), 64, 99943, jnp.int32), jax.random.randint(jax.random.fold_in(jax.random.fold_in(_rk, 2), 4), (2048,), 83, 99948, jnp.int32), jax.random.randint(jax.random.fold_in(jax.random.fold_in(_rk, 2), 5), (2048,), 54, 99999, jnp.int32), jax.random.randint(jax.random.fold_in(jax.random.fold_in(_rk, 2), 6), (2048,), 215, 99939, jnp.int32), jax.random.randint(jax.random.fold_in(jax.random.fold_in(_rk, 2), 7), (2048,), 95, 99911, jnp.int32), jax.random.randint(jax.random.fold_in(jax.random.fold_in(_rk, 2), 8), (2048,), 33, 99809, jnp.int32), jax.random.randint(jax.random.fold_in(jax.random.fold_in(_rk, 2), 9), (2048,), 67, 99845, jnp.int32), jax.random.randint(jax.random.fold_in(jax.random.fold_in(_rk, 2), 10), (2048,), 35, 99948, jnp.int32), jax.random.randint(jax.random.fold_in(jax.random.fold_in(_rk, 2), 11), (2048,), 56, 99973, jnp.int32), jax.random.randint(jax.random.fold_in(jax.random.fold_in(_rk, 2), 12), (2048,), 30, 99941, jnp.int32), jax.random.randint(jax.random.fold_in(jax.random.fold_in(_rk, 2), 13), (2048,), 97, 99859, jnp.int32), jax.random.randint(jax.random.fold_in(jax.random.fold_in(_rk, 2), 14), (2048,), 23, 99998, jnp.int32), jax.random.randint(jax.random.fold_in(jax.random.fold_in(_rk, 2), 15), (2048,), 116, 99994, jnp.int32), jax.random.randint(jax.random.fold_in(jax.random.fold_in(_rk, 2), 16), (2048,), 148, 12495, jnp.int32), jax.random.randint(jax.random.fold_in(jax.random.fold_in(_rk, 2), 17), (2048,), 206, 99747, jnp.int32), jax.random.randint(jax.random.fold_in(jax.random.fold_in(_rk, 2), 18), (2048,), 37, 99628, jnp.int32), jax.random.randint(jax.random.fold_in(jax.random.fold_in(_rk, 2), 19), (2048,), 324, 12483, jnp.int32), jax.random.randint(jax.random.fold_in(jax.random.fold_in(_rk, 2), 20), (2048,), 89, 12495, jnp.int32), jax.random.randint(jax.random.fold_in(jax.random.fold_in(_rk, 2), 21), (2048,), 68, 99881, jnp.int32), jax.random.randint(jax.random.fold_in(jax.random.fold_in(_rk, 2), 22), (2048,), 2, 99711, jnp.int32), jax.random.randint(jax.random.fold_in(jax.random.fold_in(_rk, 2), 23), (2048,), 311, 99742, jnp.int32), jax.random.randint(jax.random.fold_in(jax.random.fold_in(_rk, 2), 24), (2048,), 53, 99950, jnp.int32), jax.random.randint(jax.random.fold_in(jax.random.fold_in(_rk, 2), 25), (2048,), 190, 99982, jnp.int32), jax.random.randint(jax.random.fold_in(jax.random.fold_in(_rk, 2), 26), (2048,), 216, 99910, jnp.int32), jax.random.randint(jax.random.fold_in(jax.random.fold_in(_rk, 2), 27), (2048,), 148, 99953, jnp.int32), jax.random.randint(jax.random.fold_in(jax.random.fold_in(_rk, 2), 28), (2048,), 137, 99935, jnp.int32), jax.random.randint(jax.random.fold_in(jax.random.fold_in(_rk, 2), 29), (2048,), 122, 12485, jnp.int32), jax.random.randint(jax.random.fold_in(jax.random.fold_in(_rk, 2), 30), (2048,), 8, 99927, jnp.int32), jax.random.randint(jax.random.fold_in(jax.random.fold_in(_rk, 2), 31), (2048,), 13, 99979, jnp.int32), jax.random.randint(jax.random.fold_in(jax.random.fold_in(_rk, 2), 32), (2048,), 120, 99930, jnp.int32), jax.random.randint(jax.random.fold_in(jax.random.fold_in(_rk, 2), 33), (2048,), 49, 99972, jnp.int32), jax.random.randint(jax.random.fold_in(jax.random.fold_in(_rk, 2), 34), (2048,), 134, 99879, jnp.int32), jax.random.randint(jax.random.fold_in(jax.random.fold_in(_rk, 2), 35), (2048,), 12, 99958, jnp.int32), jax.random.randint(jax.random.fold_in(jax.random.fold_in(_rk, 2), 36), (2048,), 168, 12497, jnp.int32), jax.random.randint(jax.random.fold_in(jax.random.fold_in(_rk, 2), 37), (2048,), 57, 99894, jnp.int32), jax.random.randint(jax.random.fold_in(jax.random.fold_in(_rk, 2), 38), (2048,), 231, 99987, jnp.int32), jax.random.randint(jax.random.fold_in(jax.random.fold_in(_rk, 2), 39), (2048,), 35, 99956, jnp.int32), jax.random.randint(jax.random.fold_in(jax.random.fold_in(_rk, 2), 40), (2048,), 23, 12490, jnp.int32), jax.random.randint(jax.random.fold_in(jax.random.fold_in(_rk, 2), 41), (2048,), 114, 99951, jnp.int32), jax.random.randint(jax.random.fold_in(jax.random.fold_in(_rk, 2), 42), (2048,), 0, 99894, jnp.int32), jax.random.randint(jax.random.fold_in(jax.random.fold_in(_rk, 2), 43), (2048,), 158, 99699, jnp.int32), jax.random.randint(jax.random.fold_in(jax.random.fold_in(_rk, 2), 44), (2048,), 28, 99839, jnp.int32), jax.random.randint(jax.random.fold_in(jax.random.fold_in(_rk, 2), 45), (2048,), 5, 99956, jnp.int32), jax.random.randint(jax.random.fold_in(jax.random.fold_in(_rk, 2), 46), (2048,), 69, 99986, jnp.int32), jax.random.randint(jax.random.fold_in(jax.random.fold_in(_rk, 2), 47), (2048,), 4, 99981, jnp.int32), jax.random.randint(jax.random.fold_in(jax.random.fold_in(_rk, 2), 48), (2048,), 55, 99931, jnp.int32), jax.random.randint(jax.random.fold_in(jax.random.fold_in(_rk, 2), 49), (2048,), 82, 99978, jnp.int32)], axis=1)
        return (r_sequence_ids, r_retrieved_indices)
    r_sequence_ids, r_retrieved_indices = _rec_inputs()

    def _L0_rec_setup():
        import jax, jax.numpy as jnp
        import numpy as np
        N_ITEMS = 12500
        HIDDEN = 512
        BATCH = 1024
        SEQ_LEN = 200
        TOP_K = 50
        key = jax.random.key(seed)
        ks = jax.random.split(key, 9)
        s = 1.0 / np.sqrt(HIDDEN)
        return {'sequence_ids': jax.random.randint(ks[0], (BATCH, SEQ_LEN), 0, N_ITEMS + 1, dtype=jnp.int64 if jax.config.jax_enable_x64 else jnp.int32), 'retrieved_indices': jax.random.randint(ks[1], (BATCH, TOP_K), 0, N_ITEMS, dtype=jnp.int64 if jax.config.jax_enable_x64 else jnp.int32), 'item_embeddings': jax.random.normal(ks[2], (N_ITEMS, HIDDEN), jnp.float32) * 0.02, 'W_rec': jax.random.normal(ks[3], (HIDDEN, HIDDEN), jnp.float32) * s, 'b_rec': jnp.zeros((HIDDEN,), jnp.float32), 'gate_W': jax.random.normal(ks[4], (HIDDEN, 2 * HIDDEN), jnp.float32) * s, 'gate_b': jnp.zeros((HIDDEN,), jnp.float32), 'proj_W': jax.random.normal(ks[5], (N_ITEMS, HIDDEN), jnp.float32) * s, 'proj_b': jnp.zeros((N_ITEMS,), jnp.float32)}
    _L0_rec_all = _L0_rec_setup()
    _L0_rec_in = {k: v for k, v in _L0_rec_all.items() if k in ('item_embeddings', 'W_rec', 'b_rec', 'gate_W', 'gate_b', 'proj_W', 'proj_b')}
    del _L0_rec_all
    return {'r_sequence_ids': r_sequence_ids, 'r_retrieved_indices': r_retrieved_indices, 'L0_rec_item_embeddings': _L0_rec_in['item_embeddings'], 'L0_rec_W_rec': _L0_rec_in['W_rec'], 'L0_rec_b_rec': _L0_rec_in['b_rec'], 'L0_rec_gate_W': _L0_rec_in['gate_W'], 'L0_rec_gate_b': _L0_rec_in['gate_b'], 'L0_rec_proj_W': _L0_rec_in['proj_W'], 'L0_rec_proj_b': _L0_rec_in['proj_b']}

def reference(r_sequence_ids, r_retrieved_indices, L0_rec_item_embeddings, L0_rec_W_rec, L0_rec_b_rec, L0_rec_gate_W, L0_rec_gate_b, L0_rec_proj_W, L0_rec_proj_b):
    import jax
    import jax.numpy as jnp

    def _L0_rec_ref(sequence_ids, retrieved_indices, item_embeddings, W_rec, b_rec, gate_W, gate_b, proj_W, proj_b):
        import jax, jax.numpy as jnp
        import numpy as np
        N_ITEMS = 12500
        HIDDEN = 512
        BATCH = 1024
        SEQ_LEN = 200
        TOP_K = 50
        mask = (sequence_ids != 0)[..., None]
        gathered = item_embeddings[jnp.clip(sequence_ids - 1, 0)]
        seq_emb = jnp.where(mask, gathered, 0.0)
        denom = jnp.maximum(mask.sum(axis=1), 1).astype(seq_emb.dtype)
        pooled = seq_emb.sum(axis=1) / denom
        user_rep = pooled @ W_rec.T + b_rec
        retrieved = item_embeddings[retrieved_indices].mean(axis=1)
        concat = jnp.concatenate([user_rep, retrieved], axis=1)
        gate = jax.nn.sigmoid(concat @ gate_W.T + gate_b)
        fused = gate * user_rep + (1.0 - gate) * retrieved
        logits = fused @ proj_W.T + proj_b
        return logits
    y = _L0_rec_ref(r_sequence_ids, r_retrieved_indices, L0_rec_item_embeddings, L0_rec_W_rec, L0_rec_b_rec, L0_rec_gate_W, L0_rec_gate_b, L0_rec_proj_W, L0_rec_proj_b)
    return y

_drawn_inputs = setup_inputs


def setup_inputs(seed=0):
    import zlib

    import numpy as np

    out = dict(_drawn_inputs(seed))
    spreads = {'L0_rec_b_rec': (0.0, 0.1), 'L0_rec_gate_b': (0.0, 0.344), 'L0_rec_proj_b': (0.0, 0.1)}
    factors = {}
    for name, (base, spread) in spreads.items():
        noise = np.random.default_rng([zlib.crc32(name.encode()), seed]).standard_normal(out[name].shape)
        drawn = base * np.exp(spread * noise) if base else spread * noise
        out[name] = jnp.asarray(drawn.astype(out[name].dtype))
    for name, factor in factors.items():
        out[name] = (out[name] * factor).astype(out[name].dtype)
    return out
```

```python
from contextlib import ExitStack

import concourse.bass as bass
from concourse import mybir

F32 = mybir.dt.float32
F16 = mybir.dt.float16
I32 = mybir.dt.int32
ALU = mybir.AluOpType
ACT = mybir.ActivationFunctionType
AX = mybir.AxisListType

P = 128
STEPS = 8
SLOTS = 4
QUAD = 4
ABSENT = 512.0
F16_TOP = 14
EXP_BIAS = 127


class Plan:

    def __init__(self, seq_len, top_k, users, items, hidden):
        self.seq_len, self.top_k = seq_len, top_k
        self.users, self.items, self.hidden = users, items, hidden
        self.blocks = users // P
        self.kh = hidden // P
        self.chunks = -(-items // P)
        self.low_seq = seq_len - P
        self.ring_chunks = (self.chunks - 2) // (STEPS * SLOTS)
        assert self.ring_chunks * STEPS * SLOTS + 2 == self.chunks
        self.prep_chunks = next(n for n in range(8, 0, -1) if self.chunks % (2 * n) == 0)
        self.prep_rounds = self.chunks // (2 * self.prep_chunks)
        self.width = next(n for n in range(512, 0, -1) if items % n == 0)
        self.strips = items // self.width
        self.quads = P // QUAD
        self.max_rounds = 8
        self.early_quads = self.quads - 2 * (self.prep_rounds + self.max_rounds)
        assert self.early_quads >= 0 and self.early_quads % 2 == 0
        assert users % (8 * P) == 0 and hidden == 512 and (hidden // P * items) % (2 * self.max_rounds) == 0
        self.max_cols = hidden // P * items // (2 * self.max_rounds)


def pooling_program(nc, pl, ids, emb, w_rec_t, b_rec, w_gate_t, b_gate, proj_t, proj_b, emb_parts, fused_parts, out):
    NB, KH, NQ, H = pl.blocks, pl.kh, pl.chunks, pl.hidden
    RC = pl.ring_chunks
    TC = 2 * NQ
    PAIR = QUAD // 2
    PAIRS = P // PAIR
    ROW_U, CH_U, ROW_L, CH_L = 0, P, P + NQ, 2 * P + NQ
    HOT = 2 * P + NQ + TC

    with ExitStack() as outer:
        def sem(name):
            return outer.enter_context(nc.semaphore(name))

        def sb(name, shape, dt, scope=outer):
            return scope.enter_context(nc.sbuf_tensor(name, shape, dt))

        counts = sb("counts", [P, 2, TC, P], F16)
        hots = sb("hots", [P, 2, QUAD, HOT], F16)
        columns = sb("columns", [P, TC], F16)
        columns_i = sb("columns_i", [P, TC], I32)
        raw_ids = sb("raw_ids", [P, 2, P], I32)
        clamped = sb("clamped", [P, 2, P], I32)
        shifted = sb("shifted", [P, 2, P], F32)
        parts_i = sb("parts_i", [P, 2, P], I32)
        absent = sb("absent", [P, 2, P], F32)
        row_of = sb("row_of", [P, 2, P], F32)
        chunk_of = sb("chunk_of", [P, 2, P], F32)
        present = sb("present", [P, 2, P], F16)
        wrap = sb("wrap", [P, 1], F32)
        shift = sb("shift", [P, 1], F32)
        masked = sb("masked", [P, 1], F32)
        unused = sb("unused", [P, 1], F32)
        ret_col = sb("ret_col", [P, 1], F32)
        is_seq = sb("is_seq", [P, 2], F16)
        emb_peak = sb("emb_peak", [P, 2 * pl.prep_rounds], F32)
        proj_peak = sb("proj_peak", [P, 2 * pl.max_rounds], F32)
        peak = sb("peak", [P, 2], F32)
        peak_all = sb("peak_all", [P, 2], F32)
        expo = sb("expo", [P, 2], I32)
        scale = sb("scale", [P, 2], F32)
        unscale = sb("unscale", [P, 2], F32)
        pool_scale = sb("pool_scale", [P, NB], F32)
        ret_scale = sb("ret_scale", [P, 1], F32)
        present_n = sb("present_n", [P, 1], F32)
        present_r = sb("present_r", [P, 1], F32)
        out_scale = sb("out_scale", [P, NB], F32)

        count_ps = outer.enter_context(nc.psum_tensor("count_ps", [P, 2, 512], F32))
        pooled_ps = outer.enter_context(nc.psum_tensor("pooled_ps", [P, 4, 512], F32))
        turned_ps = outer.enter_context(nc.psum_tensor("turned_ps", [P, 512], F32))
        dense_ps = outer.enter_context(nc.psum_tensor("dense_ps", [P, 512], F32))
        turned_half = turned_ps[:].bitcast(F16)
        present_ps = dense_ps[:, 0:1]

        ids_in = sem("ids_in")
        consts_made = sem("consts_made")
        columns_made = sem("columns_made")
        stage_in = [sem(f"stage_in{s}") for s in range(2)]
        stage_free = [sem(f"stage_free{s}") for s in range(2)]
        peak_made = sem("peak_made")
        peak_spread = sem("peak_spread")
        scale_made = sem("scale_made")
        high_made = [sem(f"high_made{s}") for s in range(2)]
        split_made = [sem(f"split_made{s}") for s in range(2)]
        split_stored = [sem(f"split_stored{s}") for s in range(2)]
        ids_ready = sem("ids_ready")
        present_counted = sem("present_counted")
        pool_scale_made = sem("pool_scale_made")
        hots_made = sem("hots_made")
        pair_counted = sem("pair_counted")
        pair_moved = sem("pair_moved")

        def prepare_ids(dve, block):
            dve.wait_ge(ids_in, 16 * (block + 1))
            dve.tensor_scalar(absent[:, 1, :], raw_ids[:, 1, :], 0.0, wrap[:, 0:1], ALU.is_lt, ALU.mult)
            dve.tensor_scalar(shifted[:, 0, :], raw_ids[:, 0, :], -1.0, None, ALU.add)
            dve.drain()
            dve.scalar_tensor_tensor(shifted[:, 1, :], raw_ids[:, 1, :], shift[:, 0:1], absent[:, 1, :],
                                     ALU.add, ALU.add)
            dve.drain()
            dve.tensor_scalar(clamped[:], shifted[:], 0.0, float(pl.items - 1), ALU.max, ALU.min)
            dve.tensor_scalar(absent[:, 0, :], raw_ids[:, 0, :], 0.0, ABSENT, ALU.is_equal, ALU.mult)
            dve.tensor_scalar(absent[:, 1, :], raw_ids[:, 1, :], 0.0, masked[:, 0:1], ALU.is_equal, ALU.mult)
            dve.drain()
            dve.tensor_scalar(absent[:, 1, :], absent[:, 1, :], unused[:, 0:1], None, ALU.add)
            dve.tensor_scalar(parts_i[:], clamped[:], P - 1, None, ALU.bitwise_and)
            dve.drain()
            dve.tensor_tensor(row_of[:], parts_i[:], absent[:], ALU.add)
            dve.drain()
            dve.tensor_scalar(parts_i[:], clamped[:], 7, None, ALU.logical_shift_right)
            dve.wait_ge(present_counted, block + 1)
            dve.tensor_scalar(present[:], raw_ids[:], 0.0, None, ALU.not_equal)
            dve.drain()
            dve.tensor_copy(chunk_of[:, 0, :], parts_i[:, 0, :])
            dve.tensor_scalar(chunk_of[:, 1, :], parts_i[:, 1, :], ret_col[:, 0:1], None, ALU.add)
            dve.drain().then_inc(ids_ready, 1)

        def count_present(pe, block):
            pe.wait_ge(ids_ready, block + 1)
            if not (isinstance(block, int) and block == 0):
                pe.wait_ge(pool_scale_made, block)
            pe.matmul(present_ps, present[:, 0, :], is_seq[:, 0:1], start=True, stop=False)
            pe.matmul(present_ps, present[:, 1, :], is_seq[:, 1:2], start=False, stop=True)\
                .then_inc(present_counted, 1)

        def scale_pool(dve, block):
            dve.wait_ge(present_counted, block + 2)
            dve.tensor_scalar(present_n[:], present_ps, 1.0, None, ALU.max)
            dve.drain()
            dve.reciprocal(present_r[:], present_n[:])
            dve.drain()
            dve.tensor_scalar(pool_scale[:, bass.ds(block, 1)], present_r[:], unscale[:, 0:1], None, ALU.mult)
            dve.drain().then_inc(pool_scale_made, 1)

        def make_hots(dve, quad, slot, first_user):
            dve.wait_ge(pair_counted, 2 * quad + 2)
            for v in range(QUAD):
                u = bass.ds(first_user + v, 1)
                for at, n, of, part in ((ROW_U, P, row_of, 0), (CH_U, NQ, chunk_of, 0),
                                        (ROW_L, P, row_of, 1), (CH_L, TC, chunk_of, 1)):
                    last = dve.tensor_scalar(hots[:, slot, v, at:at + n], columns[:, 0:n], of[:, part, u],
                                             None, ALU.is_equal)
            last.then_inc(hots_made, 1)

        def count_quad(pe, quad, slot):
            pe.wait_ge(hots_made, quad + 1)
            for pair in range(2):
                pe.wait_ge(pair_moved, 2 * quad + pair + 1)
                for v in range(PAIR):
                    hot = hots[:, slot, pair * PAIR + v, :]
                    to = count_ps[:, pair, v * TC:(v + 1) * TC]
                    pe.matmul(to, hot[:, ROW_L:ROW_L + P], hot[:, CH_L:CH_L + TC], start=True, stop=False)
                    last = pe.matmul(to[:, 0:NQ], hot[:, ROW_U:ROW_U + P], hot[:, CH_U:CH_U + NQ],
                                     start=False, stop=True)
                last.then_inc(pair_counted, 1)

        def move_pair(act, number, bank, parity, first_user):
            act.wait_ge(pair_counted, number + 5)
            act.activation(counts[:, parity, :, bass.ds(first_user, PAIR)],
                           count_ps[:, bank, 0:PAIR * TC].rearrange("p (u c) -> p c u", u=PAIR),
                           ACT.Copy).then_inc(pair_moved, 1)

        with ExitStack() as inner:
            PC = pl.prep_chunks
            stage_cols = max(PC * H, pl.max_cols)
            stage = sb("stage", [P, 2, stage_cols], F32, inner)
            split = sb("split", [P, 2, PC, 2, H], F16, inner)
            block0 = inner.enter_context(nc.Block())
            E, M = pl.prep_rounds, pl.max_rounds

            @block0.sync
            def _(sp):
                sp.dma_start(raw_ids[:], ids[:, :, 0:P]).then_inc(ids_in, 16)
                with sp.Fori(0, E) as r:
                    for s in range(2):
                        sp.wait_ge(stage_free[s], r + 1)
                        sp.dma_start(stage[:, s, 0:PC * H], emb[:, bass.ds((r * 2 + s) * PC * H, PC * H)])\
                            .then_inc(stage_in[s], 16)
                with sp.Fori(0, M) as r:
                    for s in range(2):
                        sp.wait_ge(stage_free[s], r + (E + 1))
                        sp.dma_start(stage[:, s, 0:pl.max_cols],
                                     proj_t.rearrange("(p k) i -> p (k i)", p=P)[
                                         :, bass.ds((r * 2 + s) * pl.max_cols, pl.max_cols)])\
                            .then_inc(stage_in[s], 16)
                with sp.Fori(0, E) as r:
                    for s in range(2):
                        sp.wait_ge(stage_free[s], r + (E + M + 1))
                        sp.dma_start(stage[:, s, 0:PC * H], emb[:, bass.ds((r * 2 + s) * PC * H, PC * H)])\
                            .then_inc(stage_in[s], 16)

            @block0.gpsimd
            def _(pool):
                pool.iota(columns_i[:], [[1, TC]], base=0, channel_multiplier=0).then_inc(columns_made, 1)
                pool.memset(wrap[:], float(pl.items))
                pool.memset(shift[:], 0.0)
                pool.memset(masked[:], 0.0)
                pool.memset(unused[:], ABSENT)
                pool.memset(ret_col[:], float(NQ))
                pool.memset(is_seq[:], 1.0)
                pool.drain()

                def keep_from(tile, first, fill):
                    pool.affine_select(out=tile, in_=tile, pattern=[[0, 1]], compare_op=ALU.is_ge, fill=fill,
                                       base=-first, channel_multiplier=1)

                def keep_below(tile, end, fill):
                    pool.affine_select(out=tile, in_=tile, pattern=[[0, 1]], compare_op=ALU.is_ge, fill=fill,
                                       base=end - 1, channel_multiplier=-1)

                keep_from(wrap[:], pl.low_seq, 0.0)
                keep_from(shift[:], pl.low_seq, -1.0)
                keep_from(masked[:], pl.low_seq, ABSENT)
                keep_from(unused[:], pl.low_seq + pl.top_k, 0.0)
                keep_from(ret_col[:], pl.low_seq, 0.0)
                keep_below(is_seq[:, 1:2], pl.low_seq, 0.0)
                pool.drain().then_inc(consts_made, 1)
                pool.wait_ge(peak_made, 1)
                pool.partition_all_reduce(peak_all[:], peak[:], P, bass.bass_isa.ReduceOp.max)\
                    .then_inc(peak_spread, 1)
                with pool.Fori(0, E) as r:
                    for s in range(2):
                        pool.wait_ge(split_made[s], r + 1)
                        pool.dma_start(emb_parts[:, bass.ds((r * 2 + s) * PC * 2 * H, PC * 2 * H)],
                                       split[:, s].rearrange("p c t h -> p (c t h)"))\
                            .then_inc(split_stored[s], 16)
                for s in range(2):
                    pool.wait_ge(split_stored[s], 16 * E)

            @block0.vector
            def _(dve):
                for s in range(2):
                    dve.sem_inc(stage_free[s], 1)
                dve.wait_ge(columns_made, 1)
                dve.tensor_copy(columns[:], columns_i[:])
                dve.wait_ge(consts_made, 1)
                prepare_ids(dve, 0)
                for k in range(pl.early_quads):
                    make_hots(dve, k, k % 2, QUAD * k)
                for rounds, peaks, cols, quads, before in (
                        (E, emb_peak, PC * H, pl.early_quads, 0),
                        (M, proj_peak, pl.max_cols, pl.early_quads + 2 * E, E)):
                    with dve.Fori(0, rounds) as r:
                        for s in range(2):
                            dve.wait_ge(stage_in[s], 16 * r + 16 * (before + 1))
                            dve.tensor_reduce(peaks[:, bass.ds(r * 2 + s, 1)], stage[:, s, 0:cols], AX.X, ALU.max,
                                              apply_absolute_value=True).then_inc(stage_free[s], 1)
                            make_hots(dve, r * 2 + (s + quads), s, r * (2 * QUAD) + (s + quads) * QUAD)
                dve.drain()
                dve.tensor_reduce(peak[:, 0:1], emb_peak[:], AX.X, ALU.max)
                dve.tensor_reduce(peak[:, 1:2], proj_peak[:], AX.X, ALU.max).then_inc(peak_made, 1)
                dve.wait_ge(peak_spread, 1)
                set_scale(dve, peak_all[:], expo[:], scale[:], unscale[:])
                dve.drain().then_inc(scale_made, 1)
                dve.tensor_scalar(ret_scale[:], unscale[:, 0:1], 1.0 / pl.top_k, None, ALU.mult)
                scale_pool(dve, 0)
                with dve.Fori(0, E) as r:
                    for s in range(2):
                        dve.wait_ge(high_made[s], r + 1)
                        dve.scalar_tensor_tensor(split[:, s, :, 1, :],
                                                 stage[:, s, 0:PC * H].rearrange("p (c h) -> p c h", h=H),
                                                 scale[:, 0:1], split[:, s, :, 0, :], ALU.mult, ALU.subtract)
                        dve.drain().then_inc(split_made[s], 1)
                        dve.sem_inc(stage_free[s], 1)

            @block0.scalar
            def _(act):
                act.sem_inc(pair_moved, 2)
                with act.Fori(0, PAIRS // 2) as k:
                    for h in range(2):
                        move_pair(act, 2 * k + h, h, 0, 2 * PAIR * k + PAIR * h)
                act.wait_ge(scale_made, 1)
                def split_high(r, again):
                    for s in range(2):
                        act.wait_ge(stage_in[s], 16 * r + 16 * (E + M + 1))
                        if again:
                            act.wait_ge(split_stored[s], 16 * r)
                        act.activation(split[:, s, :, 0, :],
                                       stage[:, s, 0:PC * H].rearrange("p (c h) -> p c h", h=H),
                                       ACT.Copy, scale=scale[:, 0:1]).then_inc(high_made[s], 1)

                split_high(0, False)
                with act.Fori(1, E) as r:
                    split_high(r, True)

            @block0.tensor
            def _(pe):
                pe.sem_inc(present_counted, 1)
                pe.sem_inc(pair_counted, 4)
                pe.wait_ge(consts_made, 1)
                count_present(pe, 0)
                with pe.Fori(0, pl.quads // 2) as k:
                    for s in range(2):
                        count_quad(pe, 2 * k + s, s)



        with ExitStack() as inner:
            ring = sb("ring", [P, SLOTS, RC, 2, H], F16, inner)
            first_chunk = sb("first_chunk", [P, 2, H], F16, inner)
            last_chunk = sb("last_chunk", [P, 2, H], F16, inner)
            w_rec = sb("w_rec", [P, KH, H], F32, inner)
            w_gate = sb("w_gate", [P, 2 * KH, H], F32, inner)
            b_rec_all = sb("b_rec_all", [P, H], F32, inner)
            b_gate_all = sb("b_gate_all", [P, H], F32, inner)
            identity = sb("identity", [P, P], F32, inner)
            identity_h = sb("identity_h", [P, P], F16, inner)
            pooled = sb("pooled", [P, H], F32, inner)
            retrieved = sb("retrieved", [P, H], F32, inner)
            user_rep = sb("user_rep", [P, H], F32, inner)
            pooled_t = sb("pooled_t", [P, KH, P], F32, inner)
            user_t = sb("user_t", [P, KH, P], F32, inner)
            retrieved_t = sb("retrieved_t", [P, KH, P], F32, inner)
            gate = sb("gate", [P, H], F32, inner)
            mix = sb("mix", [P, H], F32, inner)
            halves = sb("halves", [P, 2, H], F16, inner)
            halves_t = sb("halves_t", [P, 2 * KH, P], F16, inner)
            fused_peak = sb("fused_peak", [P, 1], F32, inner)
            fused_expo = sb("fused_expo", [P, 1], I32, inner)
            fused_scale = sb("fused_scale", [P, 1], F32, inner)
            fused_unscale = sb("fused_unscale", [P, 1], F32, inner)

            weights_in = sem("weights_in")
            identity_made = sem("identity_made")
            ring_in = [sem(f"ring_in{s}") for s in range(SLOTS)]
            ring_used = [sem(f"ring_used{s}") for s in range(SLOTS)]
            first_in = sem("first_in")
            first_used = sem("first_used")
            last_in = sem("last_in")
            block_pooled = sem("block_pooled")
            sums_moved = sem("sums_moved")
            turned = sem("turned")
            turned_moved = sem("turned_moved")
            dense_done = sem("dense_done")
            dense_moved = sem("dense_moved")
            gate_made = sem("gate_made")
            mixed = sem("mixed")
            high_half = sem("high_half")
            low_half = sem("low_half")
            halves_moved = sem("halves_moved")
            fused_stored = sem("fused_stored")
            block1 = inner.enter_context(nc.Block())

            def over_blocks(eng, body):
                body(0, True, False)
                with eng.Fori(1, NB - 1) as b:
                    body(b, True, True)
                body(NB - 1, False, True)

            @block1.sync
            def _(sp):
                for to, of in ((w_rec, w_rec_t), (w_gate, w_gate_t)):
                    sp.dma_start(to[:], of.rearrange("(k p) n -> p k n", p=P)).then_inc(weights_in, 16)
                for to, of in ((b_rec_all, b_rec), (b_gate_all, b_gate)):
                    sp.dma_start(to[:], of.rearrange("(a n) -> a n", a=1).broadcast_to((P, H))).then_inc(weights_in, 16)
                parts = emb_parts.rearrange("p (c t h) -> p c t h", t=2, h=H)

                def stream(b, more, _):
                    sp.wait_ge(first_used, b + 1)
                    sp.dma_start(first_chunk[:], parts[:, 0]).then_inc(first_in, 16)
                    if more:
                        sp.wait_ge(ids_ready, b + 1)
                        sp.dma_start(raw_ids[:], ids[:, :, bass.ds(b * P + P, P)]).then_inc(ids_in, 16)
                    with sp.Fori(0, STEPS) as i:
                        for j in range(SLOTS):
                            sp.wait_ge(ring_used[j], b * STEPS + i + 1)
                            sp.dma_start(ring[:, j], parts[:, bass.ds(i * (SLOTS * RC) + (j * RC + 1), RC)])\
                                .then_inc(ring_in[j], 16)
                    sp.wait_ge(block_pooled, b + 1)
                    sp.dma_start(last_chunk[:], parts[:, NQ - 1]).then_inc(last_in, 16)

                over_blocks(sp, stream)

            @block1.gpsimd
            def _(pool):
                pool.memset(identity[:], 1.0)
                pool.drain()
                pool.affine_select(out=identity[:], in_=identity[:], pattern=[[-1, P]], compare_op=ALU.is_equal,
                                   fill=0.0, base=0, channel_multiplier=1)
                pool.drain()
                pool.tensor_copy(identity_h[:], identity[:])
                pool.drain().then_inc(identity_made, 1)

            def turn(pe, source, ident, to):
                for k in range(KH):
                    last = pe.transpose(to[:, k * P:(k + 1) * P], source[:, k * P:(k + 1) * P], ident[:])
                return last

            def pe_dense(pe, step, c, more=False):
                if step == 1:
                    pe.wait_ge(sums_moved, c * 2 + 6)
                    turn(pe, pooled, identity, turned_ps).then_inc(turned, 1)
                if step == 2:
                    pe.wait_ge(turned_moved, c * 3 + 1)
                    if more:
                        pe.wait_ge(pool_scale_made, c + 3)
                    for k in range(KH):
                        last = pe.matmul(dense_ps[:], pooled_t[:, k, :], w_rec[:, k, :],
                                         start=(k == 0), stop=(k == KH - 1))
                    last.then_inc(dense_done, 1)
                    turn(pe, retrieved, identity, turned_ps).then_inc(turned, 1)
                if step == 3:
                    pe.wait_ge(turned_moved, c * 3 + 2)
                    pe.wait_ge(dense_moved, c * 2 + 1)
                    turn(pe, user_rep, identity, turned_ps).then_inc(turned, 1)
                if step == 4:
                    pe.wait_ge(turned_moved, c * 3 + 3)
                    for k in range(2 * KH):
                        side = user_t if k < KH else retrieved_t
                        last = pe.matmul(dense_ps[:], side[:, k % KH, :], w_gate[:, k, :],
                                         start=(k == 0), stop=(k == 2 * KH - 1))
                    last.then_inc(dense_done, 1)
                if step == 7:
                    pe.wait_ge(low_half, c + 1)
                    for t in range(2):
                        last = turn(pe, halves[:, t, :], identity_h, turned_half[:, t * H:(t + 1) * H])
                    last.then_inc(turned, 1)

            def act_dense(act, step, c):
                if step == 1:
                    act.wait_ge(turned, c * 4 + 1)
                    act.activation(pooled_t[:].rearrange("p k u -> p (k u)"), turned_ps[:], ACT.Copy)\
                        .then_inc(turned_moved, 1)
                if step == 2:
                    act.wait_ge(turned, c * 4 + 2)
                    act.activation(retrieved_t[:].rearrange("p k u -> p (k u)"), turned_ps[:], ACT.Copy)\
                        .then_inc(turned_moved, 1)
                if step == 3:
                    act.wait_ge(turned, c * 4 + 3)
                    act.activation(user_t[:].rearrange("p k u -> p (k u)"), turned_ps[:], ACT.Copy)\
                        .then_inc(turned_moved, 1)
                if step == 5:
                    act.wait_ge(dense_moved, c * 2 + 2)
                    act.activation(gate[:], gate[:], ACT.Sigmoid).then_inc(gate_made, 1)
                if step == 6:
                    act.wait_ge(mixed, c + 1)
                    act.activation(halves[:, 0, :], mix[:], ACT.Copy, scale=fused_scale[:, 0:1])\
                        .then_inc(high_half, 1)
                if step == 7:
                    act.wait_ge(turned, c * 4 + 4)
                    act.wait_ge(fused_stored, c * 16 + 16)
                    act.activation(halves_t[:].rearrange("p k u -> p (k u)"), turned_half[:], ACT.Copy)\
                        .then_inc(halves_moved, 1)
                    act.wait_ge(halves_moved, c + 1)
                    act.dma_start(fused_parts[:, bass.ds(c * (2 * H), 2 * H)],
                                  halves_t[:].rearrange("p k u -> p (k u)")).then_inc(fused_stored, 16)

            def dve_dense(dve, step, c):
                if step == 2:
                    dve.wait_ge(dense_done, c * 2 + 1)
                    dve.tensor_tensor(user_rep[:], dense_ps[:], b_rec_all[:], ALU.add).then_inc(dense_moved, 1)
                if step == 4:
                    dve.wait_ge(dense_done, c * 2 + 2)
                    dve.tensor_tensor(gate[:], dense_ps[:], b_gate_all[:], ALU.add).then_inc(dense_moved, 1)
                if step == 5:
                    dve.tensor_tensor(mix[:], user_rep[:], retrieved[:], ALU.subtract)
                    dve.drain()
                    dve.wait_ge(gate_made, c + 1)
                    dve.tensor_tensor(mix[:], mix[:], gate[:], ALU.mult)
                    dve.drain()
                    dve.tensor_tensor(mix[:], mix[:], retrieved[:], ALU.add)
                    dve.drain()
                    dve.tensor_reduce(fused_peak[:], mix[:], AX.X, ALU.max, apply_absolute_value=True)
                    dve.drain()
                    set_scale(dve, fused_peak[:], fused_expo[:], fused_scale[:], fused_unscale[:])
                    dve.tensor_tensor(out_scale[:, bass.ds(c, 1)], fused_unscale[:], unscale[:, 1:2], ALU.mult)
                    dve.drain().then_inc(mixed, 1)
                if step == 6:
                    dve.wait_ge(high_half, c + 1)
                    dve.scalar_tensor_tensor(halves[:, 1, :], mix[:], fused_scale[:, 0:1], halves[:, 0, :],
                                             ALU.mult, ALU.subtract).then_inc(low_half, 1)

            def move_sums(act, c):
                act.wait_ge(block_pooled, c + 2)
                act.wait_ge(pool_scale_made, c + 1)
                act.activation(pooled[:], pooled_ps[:, bass.ds(c % 2 * 2, 1), :], ACT.Copy,
                               scale=pool_scale[:, bass.ds(c, 1)]).then_inc(sums_moved, 1)
                act.activation(retrieved[:], pooled_ps[:, bass.ds(c % 2 * 2 + 1, 1), :], ACT.Copy,
                               scale=ret_scale[:, 0:1]).then_inc(sums_moved, 1)

            @block1.tensor
            def _(pe):
                for s in ring_used + [first_used, block_pooled]:
                    pe.sem_inc(s, 1)
                pe.wait_ge(weights_in, 64)
                pe.wait_ge(identity_made, 1)

                def pool_chunk(b, chunk, parts, start, stop):
                    for t in range(2):
                        users = counts[:, bass.ds(b % 2, 1), bass.ds(chunk + t * NQ, 1), :]
                        for half in range(2):
                            last = pe.matmul(pooled_ps[:, bass.ds(b % 2 * 2 + t, 1), :], users, parts[:, half, :],
                                             start=start and half == 0, stop=stop and half == 1)
                    return last

                def pool_block(b, more, dense):
                    pe.wait_ge(pair_moved, b * PAIRS + (PAIRS + 2))
                    pe.wait_ge(sums_moved, b * 2 + 2)
                    pe.wait_ge(first_in, b * 16 + 16)
                    pool_chunk(b, 0, first_chunk, True, False).then_inc(first_used, 1)
                    with pe.Fori(0, STEPS) as i:
                        if more:
                            with pe.If(i == 0):
                                count_present(pe, b + 1)
                        if dense:
                            for step in (1, 2, 3, 4, 7):
                                with pe.If(i == step):
                                    pe_dense(pe, step, b - 1, more)
                        for j in range(SLOTS):
                            pe.wait_ge(ring_in[j], b * (16 * STEPS) + i * 16 + 16)
                            for q in range(RC):
                                last = pool_chunk(b, i * (SLOTS * RC) + (j * RC + q + 1), ring[:, j, q],
                                                  False, False)
                            last.then_inc(ring_used[j], 1)
                            if more:
                                count_quad(pe, b * pl.quads + i * SLOTS + (pl.quads + j), j % 2)
                    pe.wait_ge(last_in, b * 16 + 16)
                    pool_chunk(b, NQ - 1, last_chunk, False, True).then_inc(block_pooled, 1)

                over_blocks(pe, pool_block)
                for step in (1, 2, 3, 4, 7):
                    pe_dense(pe, step, NB - 1)

            @block1.scalar
            def _(act):
                act.sem_inc(sums_moved, 4)
                act.sem_inc(fused_stored, 16)

                def move_block(b, more, dense):
                    if dense:
                        move_sums(act, b - 1)
                    with act.Fori(0, STEPS) as i:
                        for j in range(SLOTS):
                            if more:
                                for h in range(2):
                                    move_pair(act, b * PAIRS + i * (2 * SLOTS) + (PAIRS + 2 * j + h), h, (b + 1) % 2,
                                              i * (SLOTS * QUAD) + (j * QUAD + h * PAIR))
                            if dense and j == 1:
                                for step in (1, 2, 3, 5, 6, 7):
                                    with act.If(i == step):
                                        act_dense(act, step, b - 1)

                over_blocks(act, move_block)
                move_sums(act, NB - 1)
                for step in (1, 2, 3, 5, 6, 7):
                    act_dense(act, step, NB - 1)
                act.wait_ge(fused_stored, 16 * NB + 16)

            @block1.vector
            def _(dve):
                def ready_block(b, more, dense):
                    if more:
                        prepare_ids(dve, b + 1)
                    with dve.Fori(0, STEPS) as i:
                        for j in range(SLOTS):
                            if more:
                                make_hots(dve, b * pl.quads + i * SLOTS + (pl.quads + j), j % 2,
                                          i * (SLOTS * QUAD) + j * QUAD)
                            if j == 1:
                                if more:
                                    with dve.If(i == 1):
                                        scale_pool(dve, b + 1)
                                if dense:
                                    for step in (2, 4, 5, 6):
                                        with dve.If(i == step):
                                            dve_dense(dve, step, b - 1)

                over_blocks(dve, ready_block)
                for step in (2, 4, 5, 6):
                    dve_dense(dve, step, NB - 1)

        with ExitStack() as inner:
            W = pl.width
            GROUP = 4
            fused = sb("fused", [P, NB, 2, KH, P], F16, inner)
            strip = sb("strip", [P, KH, W], F32, inner)
            strip_parts = sb("strip_parts", [P, 2, 2, KH, W], F16, inner)
            bias = sb("bias", [P, 2, W], F32, inner)
            rows = sb("rows", [P, 2, GROUP, W], F32, inner)
            logit_ps = [count_ps[:, 0], count_ps[:, 1], pooled_ps[:, 0], pooled_ps[:, 1],
                        pooled_ps[:, 2], pooled_ps[:, 3], turned_ps, dense_ps]
            fused_in = sem("fused_in")
            strip_in = sem("strip_in")
            bias_in = sem("bias_in")
            strip_high = sem("strip_high")
            strip_split = sem("strip_split")
            strip_used = sem("strip_used")
            logits_made = sem("logits_made")
            logits_moved = sem("logits_moved")
            rows_stored = [sem(f"rows_stored{s}") for s in range(2)]
            block2 = inner.enter_context(nc.Block())
            halves_n = NB // 8

            @block2.sync
            def _(sp):
                sp.dma_start(fused[:].rearrange("p b t k u -> p (b t k u)"), fused_parts).then_inc(fused_in, 16)
                for s in rows_stored:
                    sp.sem_inc(s, 16)

                def load(c):
                    cols = bass.ds(c * W, W)
                    sp.dma_start(strip[:], proj_t.rearrange("(k p) i -> p k i", p=P)[:, :, cols])\
                        .then_inc(strip_in, 16)
                    sp.dma_start(bias[:, bass.ds(c % 2, 1), :],
                                 proj_b.rearrange("(a n) -> a n", a=1)[:, cols].broadcast_to((P, W)))\
                        .then_inc(bias_in, 16)

                def store(c):
                    with sp.Fori(0, halves_n) as g:
                        for s in range(2):
                            sp.wait_ge(logits_moved, c * NB + g * 8 + (s * GROUP + GROUP + 8))
                            sp.dma_start(out.rearrange("(b p) i -> p b i", p=P)[
                                :, bass.ds(g * 8 + s * GROUP, GROUP), bass.ds(c * W, W)], rows[:, s])\
                                .then_inc(rows_stored[s], 16)

                load(0)
                with sp.Fori(0, pl.strips - 1) as c:
                    sp.wait_ge(strip_split, c + 1)
                    sp.wait_ge(logits_moved, c * NB + 8)
                    load(c + 1)
                    store(c)
                store(pl.strips - 1)
                for s in range(2):
                    sp.wait_ge(rows_stored[s], 16 * halves_n * pl.strips + 16)

            @block2.scalar
            def _(act):
                with act.Fori(0, pl.strips) as c:
                    act.wait_ge(strip_in, c * 16 + 16)
                    act.wait_ge(strip_used, c + 1)
                    act.activation(strip_parts[:, bass.ds(c % 2, 1), 0], strip[:], ACT.Copy, scale=scale[:, 1:2])\
                        .then_inc(strip_high, 1)

            @block2.vector
            def _(dve):
                dve.sem_inc(logits_moved, 8)

                def split_low(c):
                    dve.wait_ge(bias_in, c * 16 + 16)
                    dve.wait_ge(strip_high, c + 1)
                    par = bass.ds(c % 2, 1)
                    dve.scalar_tensor_tensor(strip_parts[:, par, 1], strip[:], scale[:, 1:2],
                                             strip_parts[:, par, 0], ALU.mult, ALU.subtract)\
                        .then_inc(strip_split, 1)

                def move_logits(c, more):
                    if more:
                        split_low(c + 1)
                    with dve.Fori(0, halves_n) as g:
                        for s in range(2):
                            dve.wait_ge(rows_stored[s], c * (16 * halves_n) + g * 16 + 16)
                            for v in range(GROUP):
                                bank = s * GROUP + v
                                dve.wait_ge(logits_made, c * NB + g * 8 + (bank + 1))
                                dve.scalar_tensor_tensor(rows[:, s, v, :], logit_ps[bank][:, 0:W],
                                                         out_scale[:, bass.ds(g * 8 + bank, 1)],
                                                         bias[:, bass.ds(c % 2, 1), :], ALU.mult, ALU.add)\
                                    .then_inc(logits_moved, 1)

                split_low(0)
                with dve.Fori(0, pl.strips - 1) as c:
                    move_logits(c, True)
                move_logits(pl.strips - 1, False)

            @block2.tensor
            def _(pe):
                pe.sem_inc(strip_used, 2)
                pe.wait_ge(fused_in, 16)
                with pe.Fori(0, pl.strips) as c:
                    with pe.Fori(0, halves_n) as g:
                        pe.wait_ge(strip_split, c + 1)
                        for bank in range(8):
                            pe.wait_ge(logits_moved, c * NB + g * 8 + (bank + 1))
                            for k in range(KH):
                                for n, (f, w) in enumerate(((0, 0), (0, 1), (1, 0))):
                                    last = pe.matmul(logit_ps[bank][:, 0:W],
                                                     fused[:, bass.ds(g * 8 + bank, 1), f, k, :],
                                                     strip_parts[:, bass.ds(c % 2, 1), w, k, :],
                                                     start=(k == 0 and n == 0), stop=(k == KH - 1 and n == 2))
                            last.then_inc(logits_made, 1)
                    pe.drain().then_inc(strip_used, 1)


def set_scale(dve, peak, expo, scale, unscale):
    dve.tensor_scalar(expo, peak.bitcast(I32), 23, None, ALU.logical_shift_right)
    dve.drain()
    dve.tensor_scalar(expo, expo, -1.0, float(2 * EXP_BIAS + F16_TOP), ALU.mult, ALU.add)
    dve.drain()
    dve.tensor_scalar(expo, expo, float(2 * EXP_BIAS - 1), None, ALU.min)
    dve.drain()
    dve.tensor_scalar(scale.bitcast(I32), expo, 23, None, ALU.logical_shift_left)
    dve.drain()
    dve.tensor_scalar(expo, expo, -1.0, float(2 * EXP_BIAS), ALU.mult, ALU.add)
    dve.drain()
    dve.tensor_scalar(unscale.bitcast(I32), expo, 23, None, ALU.logical_shift_left)
    dve.drain()


def kernel(r_sequence_ids, r_retrieved_indices, L0_rec_item_embeddings, L0_rec_W_rec, L0_rec_b_rec,
           L0_rec_gate_W, L0_rec_gate_b, L0_rec_proj_W, L0_rec_proj_b):
    import numpy as np
    import concourse.bacc as bacc
    from concourse.bass_utils import run_bass_kernel_spmd

    seq, ret = np.asarray(r_sequence_ids), np.asarray(r_retrieved_indices)
    table = np.asarray(L0_rec_item_embeddings)
    items, hidden = table.shape
    users, seq_len = seq.shape
    pl = Plan(seq_len, ret.shape[1], users, items, hidden)

    ids = np.zeros((P, 2, users), seq.dtype)
    ids[:, 0] = seq.T[:P]
    ids[:pl.low_seq, 1] = seq.T[P:]
    ids[pl.low_seq:pl.low_seq + pl.top_k, 1] = ret.T
    emb = np.zeros((pl.chunks * P, hidden), table.dtype)
    emb[:items] = table
    emb = np.ascontiguousarray(emb.reshape(pl.chunks, P, hidden).transpose(1, 0, 2)).reshape(P, -1)

    arrays = {
        "ids": ids, "emb": emb,
        "w_rec_t": np.ascontiguousarray(np.asarray(L0_rec_W_rec).T), "b_rec": np.asarray(L0_rec_b_rec),
        "w_gate_t": np.ascontiguousarray(np.asarray(L0_rec_gate_W).T), "b_gate": np.asarray(L0_rec_gate_b),
        "proj_t": np.ascontiguousarray(np.asarray(L0_rec_proj_W).T), "proj_b": np.asarray(L0_rec_proj_b),
    }
    nc = bacc.Bacc("TRN2", target_bir_lowering=False, num_devices=1)
    args = [nc.dram_tensor(name, a.shape, mybir.dt.from_np(a.dtype), kind="ExternalInput").ap()
            for name, a in arrays.items()]
    emb_parts = nc.dram_tensor("emb_parts", (P, pl.chunks * 2 * hidden), F16, kind="Internal").ap()
    fused_parts = nc.dram_tensor("fused_parts", (P, pl.blocks * 2 * hidden), F16, kind="Internal").ap()
    out = nc.dram_tensor("logits", (users, items), F32, kind="ExternalOutput").ap()
    pooling_program(nc, pl, *args, emb_parts, fused_parts, out)
    result = run_bass_kernel_spmd(nc, [arrays], core_ids=[0])
    return result.results[0]["logits"]
```

```python
from contextlib import ExitStack

import concourse.bass as bass
from concourse import mybir

F32 = mybir.dt.float32
F16 = mybir.dt.float16
I32 = mybir.dt.int32
ALU = mybir.AluOpType
ACT = mybir.ActivationFunctionType
AX = mybir.AxisListType

P = 128
STEPS = 8
SLOTS = 4
QUAD = 4
DVE_DENSE_AT = {2: (3, 1), 4: (5, 2), 5: (6, 3), 6: (7, 2)}
ABSENT = 512.0
F16_TOP = 14
EXP_BIAS = 127


class Plan:

    def __init__(self, seq_len, top_k, users, items, hidden):
        self.seq_len, self.top_k = seq_len, top_k
        self.users, self.items, self.hidden = users, items, hidden
        self.blocks = users // P
        self.kh = hidden // P
        self.chunks = -(-items // P)
        self.low_seq = seq_len - P
        self.ring_chunks = (self.chunks - 2) // (STEPS * SLOTS)
        assert self.ring_chunks * STEPS * SLOTS + 2 == self.chunks
        self.prep_chunks = next(n for n in range(8, 0, -1) if self.chunks % (2 * n) == 0)
        self.prep_rounds = self.chunks // (2 * self.prep_chunks)
        self.width = next(n for n in range(512, 0, -1) if items % n == 0)
        self.strips = items // self.width
        self.quads = P // QUAD
        self.piece_quads = 2
        assert self.quads == STEPS * SLOTS and self.quads >= 2 * self.prep_rounds * self.piece_quads
        assert users % (8 * P) == 0 and hidden == 512
        self.looks = (self.blocks - 1) * STEPS
        self.look_step = hidden // P * items // self.looks
        self.look_cols = hidden // P * items - self.look_step * (self.looks - 1)


def pooling_program(nc, pl, ids, emb, w_rec_t, b_rec, w_gate_t, b_gate, proj_t, proj_b, emb_parts, fused_parts, out):
    NB, KH, NQ, H = pl.blocks, pl.kh, pl.chunks, pl.hidden
    RC = pl.ring_chunks
    TC = 2 * NQ
    PAIR = QUAD // 2
    PAIRS = P // PAIR
    ROW_U, CH_U, ROW_L, CH_L = 0, P, P + NQ, 2 * P + NQ
    HOT = 2 * P + NQ + TC

    with ExitStack() as outer:
        def sem(name):
            return outer.enter_context(nc.semaphore(name))

        def sb(name, shape, dt, scope=outer):
            return scope.enter_context(nc.sbuf_tensor(name, shape, dt))

        counts = sb("counts", [P, 2, TC, P], F16)
        hots = sb("hots", [P, SLOTS, QUAD, HOT], F16)
        columns = sb("columns", [P, TC], F16)
        raw_ids = sb("raw_ids", [P, 2, P], I32)
        clamped = sb("clamped", [P, 2, P], I32)
        shifted = sb("shifted", [P, 2, P], F32)
        parts_i = sb("parts_i", [P, 2, P], I32)
        absent = sb("absent", [P, 2, P], F32)
        row_of = sb("row_of", [P, 2, P], F32)
        chunk_of = sb("chunk_of", [P, 2, P], F32)
        present = sb("present", [P, 2, P], F16)
        wrap = sb("wrap", [P, 1], F32)
        shift = sb("shift", [P, 1], F32)
        masked = sb("masked", [P, 1], F32)
        unused = sb("unused", [P, 1], F32)
        ret_col = sb("ret_col", [P, 1], F32)
        is_seq = sb("is_seq", [P, 2], F16)
        emb_norm = sb("emb_norm", [P, 2 * pl.prep_rounds], F32)
        proj_norm = sb("proj_norm", [P, pl.looks], F32)
        norm = sb("norm", [P, 2], F32)
        norm_all = sb("norm_all", [P, 2], F32)
        expo = sb("expo", [P, 2], I32)
        scale = sb("scale", [P, 2], F32)
        unscale = sb("unscale", [P, 2], F32)
        pool_scale = sb("pool_scale", [P, NB], F32)
        ret_scale = sb("ret_scale", [P, 1], F32)
        warm = sb("warm", [P, 1], F32)
        present_n = sb("present_n", [P, 1], F32)
        present_r = sb("present_r", [P, 1], F32)
        fused_unscale = sb("fused_unscale", [P, NB], F32)
        out_scale = sb("out_scale", [P, NB], F32)

        count_ps = outer.enter_context(nc.psum_tensor("count_ps", [P, 2, 512], F32))
        pooled_ps = outer.enter_context(nc.psum_tensor("pooled_ps", [P, 4, 512], F32))
        turned_ps = outer.enter_context(nc.psum_tensor("turned_ps", [P, 512], F32))
        dense_ps = outer.enter_context(nc.psum_tensor("dense_ps", [P, 512], F32))
        turned_half = turned_ps[:].bitcast(F16)
        present_ps = dense_ps[:, 0:1]

        ids_in = sem("ids_in")
        consts_made = sem("consts_made")
        columns_made = sem("columns_made")
        stage_in = [sem(f"stage_in{s}") for s in range(2)]
        stage_free = [sem(f"stage_free{s}") for s in range(2)]
        pieces_summed = sem("pieces_summed")
        norm_made = sem("norm_made")
        norm_spread = sem("norm_spread")
        scale_made = sem("scale_made")
        ids_ready = sem("ids_ready")
        present_counted = sem("present_counted")
        pool_scale_made = sem("pool_scale_made")
        hots_made = sem("hots_made")
        pair_counted = sem("pair_counted")
        pair_moved = sem("pair_moved")

        def prepare_ids(dve, block):
            dve.wait_ge(ids_in, 16 * (block + 1))
            dve.tensor_scalar(absent[:, 1, :], raw_ids[:, 1, :], 0.0, wrap[:, 0:1], ALU.is_lt, ALU.mult)
            dve.tensor_scalar(shifted[:, 0, :], raw_ids[:, 0, :], -1.0, None, ALU.add)
            dve.drain()
            dve.scalar_tensor_tensor(shifted[:, 1, :], raw_ids[:, 1, :], shift[:, 0:1], absent[:, 1, :],
                                     ALU.add, ALU.add)
            dve.drain()
            dve.tensor_scalar(clamped[:], shifted[:], 0.0, float(pl.items - 1), ALU.max, ALU.min)
            dve.tensor_scalar(absent[:, 0, :], raw_ids[:, 0, :], 0.0, ABSENT, ALU.is_equal, ALU.mult)
            dve.tensor_scalar(absent[:, 1, :], raw_ids[:, 1, :], 0.0, masked[:, 0:1], ALU.is_equal, ALU.mult)
            dve.drain()
            dve.tensor_scalar(absent[:, 1, :], absent[:, 1, :], unused[:, 0:1], None, ALU.add)
            dve.tensor_scalar(parts_i[:], clamped[:], P - 1, None, ALU.bitwise_and)
            dve.drain()
            dve.tensor_tensor(row_of[:], parts_i[:], absent[:], ALU.add)
            dve.drain()
            dve.tensor_scalar(parts_i[:], clamped[:], 7, None, ALU.logical_shift_right)
            dve.wait_ge(present_counted, block + 1)
            dve.tensor_scalar(present[:], raw_ids[:], 0.0, None, ALU.not_equal)
            dve.drain()
            dve.tensor_copy(chunk_of[:, 0, :], parts_i[:, 0, :])
            dve.tensor_scalar(chunk_of[:, 1, :], parts_i[:, 1, :], ret_col[:, 0:1], None, ALU.add)
            dve.drain().then_inc(ids_ready, 1)

        def count_present(pe, block):
            pe.wait_ge(ids_ready, block + 1)
            if not (isinstance(block, int) and block == 0):
                pe.wait_ge(pool_scale_made, block)
            pe.matmul(present_ps, present[:, 0, :], is_seq[:, 0:1], start=True, stop=False)
            pe.matmul(present_ps, present[:, 1, :], is_seq[:, 1:2], start=False, stop=True)\
                .then_inc(present_counted, 1)

        def scale_pool(dve, block):
            dve.wait_ge(present_counted, block + 2)
            dve.tensor_scalar(present_n[:], present_ps, 1.0, None, ALU.max)
            dve.drain()
            dve.reciprocal(present_r[:], present_n[:])
            dve.drain()
            dve.tensor_scalar(pool_scale[:, bass.ds(block, 1)], present_r[:], unscale[:, 0:1], None, ALU.mult)
            dve.drain().then_inc(pool_scale_made, 1)

        def make_hots(dve, quad, slot, first_user):
            dve.wait_ge(pair_counted, 2 * quad + 2)
            for v in range(QUAD):
                u = bass.ds(first_user + v, 1)
                for at, n, of, part in ((ROW_U, P, row_of, 0), (CH_U, NQ, chunk_of, 0),
                                        (ROW_L, P, row_of, 1), (CH_L, TC, chunk_of, 1)):
                    last = dve.tensor_scalar(hots[:, slot, v, at:at + n], columns[:, 0:n], of[:, part, u],
                                             None, ALU.is_equal)
            last.then_inc(hots_made, 1)

        def count_quad(pe, quad, slot):
            pe.wait_ge(hots_made, quad + 1)
            for pair in range(2):
                pe.wait_ge(pair_moved, 2 * quad + pair + 1)
                for v in range(PAIR):
                    hot = hots[:, slot, pair * PAIR + v, :]
                    to = count_ps[:, pair, v * TC:(v + 1) * TC]
                    pe.matmul(to, hot[:, ROW_L:ROW_L + P], hot[:, CH_L:CH_L + TC], start=True, stop=False)
                    last = pe.matmul(to[:, 0:NQ], hot[:, ROW_U:ROW_U + P], hot[:, CH_U:CH_U + NQ],
                                     start=False, stop=True)
                last.then_inc(pair_counted, 1)

        def move_pair(act, number, bank, parity, first_user):
            act.wait_ge(pair_counted, number + (2 * SLOTS + 1))
            act.activation(counts[:, parity, :, bass.ds(first_user, PAIR)],
                           count_ps[:, bank, 0:PAIR * TC].rearrange("p (u c) -> p c u", u=PAIR),
                           ACT.Copy).then_inc(pair_moved, 1)

        with ExitStack() as inner:
            PC = pl.prep_chunks
            E = pl.prep_rounds
            PQ = pl.piece_quads
            columns_i = sb("columns_i", [P, TC], I32, inner)
            stage = sb("stage", [P, 2, PC * H], F32, inner)
            block0 = inner.enter_context(nc.Block())

            @block0.sync
            def _(sp):
                sp.dma_start(raw_ids[:], ids[:, :, 0:P]).then_inc(ids_in, 16)
                with sp.Fori(0, E) as r:
                    for s in range(2):
                        sp.wait_ge(stage_free[s], r + 1)
                        sp.dma_start(stage[:, s, :], emb[:, bass.ds((r * 2 + s) * PC * H, PC * H)])\
                            .then_inc(stage_in[s], 16)

            @block0.gpsimd
            def _(pool):
                pool.iota(columns_i[:], [[1, TC]], base=0, channel_multiplier=0).then_inc(columns_made, 1)
                pool.memset(wrap[:], float(pl.items))
                pool.memset(shift[:], 0.0)
                pool.memset(masked[:], 0.0)
                pool.memset(unused[:], ABSENT)
                pool.memset(ret_col[:], float(NQ))
                pool.memset(is_seq[:], 1.0)
                pool.drain()

                def keep_from(tile, first, fill):
                    pool.affine_select(out=tile, in_=tile, pattern=[[0, 1]], compare_op=ALU.is_ge, fill=fill,
                                       base=-first, channel_multiplier=1)

                def keep_below(tile, end, fill):
                    pool.affine_select(out=tile, in_=tile, pattern=[[0, 1]], compare_op=ALU.is_ge, fill=fill,
                                       base=end - 1, channel_multiplier=-1)

                keep_from(wrap[:], pl.low_seq, 0.0)
                keep_from(shift[:], pl.low_seq, -1.0)
                keep_from(masked[:], pl.low_seq, ABSENT)
                keep_from(unused[:], pl.low_seq + pl.top_k, 0.0)
                keep_from(ret_col[:], pl.low_seq, 0.0)
                keep_below(is_seq[:, 1:2], pl.low_seq, 0.0)
                pool.drain().then_inc(consts_made, 1)
                pool.wait_ge(norm_made, 1)
                pool.partition_all_reduce(norm_all[:, 0:1], norm[:, 0:1], P, bass.bass_isa.ReduceOp.max)\
                    .then_inc(norm_spread, 1)

            @block0.vector
            def _(dve):
                dve.wait_ge(columns_made, 1)
                dve.tensor_copy(columns[:], columns_i[:])
                dve.wait_ge(consts_made, 1)
                prepare_ids(dve, 0)
                with dve.Fori(0, STEPS) as i:
                    for j in range(SLOTS):
                        make_hots(dve, i * SLOTS + j, j, i * (SLOTS * QUAD) + j * QUAD)
                dve.wait_ge(pieces_summed, 2 * E)
                dve.tensor_reduce(norm[:, 0:1], emb_norm[:], AX.X, ALU.add).then_inc(norm_made, 1)
                dve.wait_ge(norm_spread, 1)
                scale_from_squares(dve, norm_all[:, 0:1], expo[:, 0:1], scale[:, 0:1], unscale[:, 0:1])
                dve.drain().then_inc(scale_made, 1)
                dve.tensor_scalar(ret_scale[:], unscale[:, 0:1], 1.0 / pl.top_k, None, ALU.mult)
                scale_pool(dve, 0)

            @block0.scalar
            def _(act):
                act.wait_ge(consts_made, 1)
                act.activation(warm[:], unused[:], ACT.Sigmoid)
                act.sem_inc(pair_moved, 2)
                for s in range(2):
                    act.sem_inc(stage_free[s], 1)
                with act.Fori(0, E) as r:
                    for s in range(2):
                        act.wait_ge(stage_in[s], 16 * r + 16)
                        act.activation(stage[:, s, :], stage[:, s, :], ACT.Square,
                                       accum_out=emb_norm[:, bass.ds(r * 2 + s, 1)]).then_inc(pieces_summed, 1)
                        act.drain().then_inc(stage_free[s], 1)
                        for k in range(2 * PQ):
                            move_pair(act, r * (4 * PQ) + (2 * PQ * s + k), k % 2, 0,
                                      r * (4 * PQ * PAIR) + (2 * PQ * s + k) * PAIR)
                for m in range(4 * PQ * E, PAIRS):
                    move_pair(act, m, m % 2, 0, m * PAIR)

            @block0.tensor
            def _(pe):
                pe.sem_inc(present_counted, 1)
                pe.sem_inc(pair_counted, 2 * SLOTS)
                pe.wait_ge(consts_made, 1)
                count_present(pe, 0)
                with pe.Fori(0, STEPS) as i:
                    for j in range(SLOTS):
                        count_quad(pe, i * SLOTS + j, j)

        with ExitStack() as inner:
            ring = sb("ring", [P, SLOTS, RC, 2, H], F16, inner)
            first_chunk = sb("first_chunk", [P, 2, H], F16, inner)
            last_chunk = sb("last_chunk", [P, 2, H], F16, inner)
            w_rec = sb("w_rec", [P, KH, H], F32, inner)
            w_gate = sb("w_gate", [P, 2 * KH, H], F32, inner)
            b_rec_all = sb("b_rec_all", [P, H], F32, inner)
            b_gate_all = sb("b_gate_all", [P, H], F32, inner)
            identity = sb("identity", [P, P], F32, inner)
            identity_h = sb("identity_h", [P, P], F16, inner)
            pooled = sb("pooled", [P, H], F32, inner)
            retrieved = sb("retrieved", [P, H], F32, inner)
            user_rep = sb("user_rep", [P, H], F32, inner)
            pooled_t = sb("pooled_t", [P, KH, P], F32, inner)
            user_t = sb("user_t", [P, KH, P], F32, inner)
            retrieved_t = sb("retrieved_t", [P, KH, P], F32, inner)
            gate = sb("gate", [P, H], F32, inner)
            mix = sb("mix", [P, H], F32, inner)
            halves = sb("halves", [P, 2, H], F16, inner)
            halves_t = sb("halves_t", [P, 2 * KH, P], F16, inner)
            fused_peak = sb("fused_peak", [P, 1], F32, inner)
            fused_expo = sb("fused_expo", [P, 1], I32, inner)
            fused_scale = sb("fused_scale", [P, 1], F32, inner)
            fused_unscale_1 = sb("fused_unscale_1", [P, 1], F32, inner)
            look = sb("look", [P, pl.look_cols], F32, inner)
            def stage32(s):
                return w_gate[:, s * KH:s * KH + RC, :]

            edges32 = (w_gate[:, RC, :], w_gate[:, KH + RC, :])
            assert RC < KH

            weights_in = sem("weights_in")
            gate_weights_in = sem("gate_weights_in")
            edges_in = sem("edges_in")
            edges_high = sem("edges_high")
            edges_made = sem("edges_made")
            edges_stored = sem("edges_stored")
            high_made = sem("high_made")
            parts_made = sem("parts_made")
            chunks_in = [sem(f"chunks_in{s}") for s in range(2)]
            ring_stored = [sem(f"ring_stored{s}") for s in range(SLOTS)]
            look_in = sem("look_in")
            look_done = sem("look_done")
            identity_made = sem("identity_made")
            ring_in = [sem(f"ring_in{s}") for s in range(SLOTS)]
            ring_used = [sem(f"ring_used{s}") for s in range(SLOTS)]
            first_in = sem("first_in")
            first_used = sem("first_used")
            last_in = sem("last_in")
            block_pooled = sem("block_pooled")
            sums_moved = sem("sums_moved")
            turned = sem("turned")
            turned_moved = sem("turned_moved")
            dense_done = sem("dense_done")
            dense_moved = sem("dense_moved")
            gate_made = sem("gate_made")
            mixed = sem("mixed")
            high_half = sem("high_half")
            low_half = sem("low_half")
            halves_moved = sem("halves_moved")
            fused_stored = sem("fused_stored")
            block1 = inner.enter_context(nc.Block())

            def over_blocks(eng, body):
                body(0, True, False)
                with eng.Fori(1, NB - 1) as b:
                    body(b, True, True)
                body(NB - 1, False, True)

            @block1.sync
            def _(sp):
                parts = emb_parts.rearrange("p (c t h) -> p c t h", t=2, h=H)
                table = emb.rearrange("p (c h) -> p c h", h=H)
                def next_ids(b):
                    sp.wait_ge(ids_ready, b + 1)
                    sp.dma_start(raw_ids[:], ids[:, :, bass.ds(b * P + P, P)]).then_inc(ids_in, 16)

                def stream_table():
                    for to, chunk in zip(edges32, (0, NQ - 1)):
                        sp.dma_start(to, table[:, chunk]).then_inc(edges_in, 16)
                    next_ids(0)
                    with sp.Fori(0, STEPS) as i:
                        for j in range(SLOTS):
                            sp.wait_ge(parts_made, i * SLOTS + (j + 1))
                            sp.dma_start(stage32(j % 2), table[:, bass.ds(i * (SLOTS * RC) + (j * RC + 1), RC)])\
                                .then_inc(chunks_in[j % 2], 16)
                    sp.dma_start(w_rec[:], w_rec_t.rearrange("(k p) n -> p k n", p=P)).then_inc(weights_in, 16)
                    for to, of in ((b_rec_all, b_rec), (b_gate_all, b_gate)):
                        sp.dma_start(to[:], of.rearrange("(a n) -> a n", a=1).broadcast_to((P, H)))\
                            .then_inc(weights_in, 16)
                    sp.wait_ge(parts_made, STEPS * SLOTS + 2)
                    sp.wait_ge(edges_made, 1)
                    sp.dma_start(w_gate[:], w_gate_t.rearrange("(k p) n -> p k n", p=P)).then_inc(gate_weights_in, 16)
                    sp.wait_ge(edges_stored, 32)
                    for j in range(SLOTS):
                        sp.wait_ge(ring_stored[j], 16 * STEPS)

                def stream(b, more, later):
                    if not later:
                        return stream_table()
                    sp.wait_ge(first_used, b + 1)
                    sp.dma_start(first_chunk[:], parts[:, 0]).then_inc(first_in, 16)
                    if more:
                        next_ids(b)
                    with sp.Fori(0, STEPS) as i:
                        for j in range(SLOTS):
                            sp.wait_ge(ring_used[j], b * STEPS + i + 1)
                            sp.dma_start(ring[:, j], parts[:, bass.ds(i * (SLOTS * RC) + (j * RC + 1), RC)])\
                                .then_inc(ring_in[j], 16)
                    sp.wait_ge(block_pooled, b + 1)
                    sp.dma_start(last_chunk[:], parts[:, NQ - 1]).then_inc(last_in, 16)

                over_blocks(sp, stream)

            @block1.gpsimd
            def _(pool):
                pool.memset(identity[:], 1.0)
                pool.drain()
                pool.affine_select(out=identity[:], in_=identity[:], pattern=[[-1, P]], compare_op=ALU.is_equal,
                                   fill=0.0, base=0, channel_multiplier=1)
                pool.drain()
                pool.tensor_copy(identity_h[:], identity[:])
                pool.drain().then_inc(identity_made, 1)
                parts = emb_parts.rearrange("p (c t h) -> p c t h", t=2, h=H)
                pool.wait_ge(edges_made, 1)
                pool.dma_start(parts[:, 0], first_chunk[:]).then_inc(edges_stored, 16)
                pool.dma_start(parts[:, NQ - 1], last_chunk[:]).then_inc(edges_stored, 16)
                with pool.Fori(0, STEPS) as i:
                    for j in range(SLOTS):
                        pool.wait_ge(parts_made, i * SLOTS + (j + 3))
                        pool.dma_start(parts[:, bass.ds(i * (SLOTS * RC) + (j * RC + 1), RC)], ring[:, j])\
                            .then_inc(ring_stored[j], 16)
                looked = proj_t.rearrange("(p k) i -> p (k i)", p=P)
                with pool.Fori(0, pl.looks) as n:
                    pool.wait_ge(look_done, n + 1)
                    pool.dma_start(look[:], looked[:, bass.ds(n * pl.look_step, pl.look_cols)]).then_inc(look_in, 16)
                pool.wait_ge(norm_made, 2)
                pool.partition_all_reduce(norm_all[:, 1:2], norm[:, 1:2], P, bass.bass_isa.ReduceOp.max)\
                    .then_inc(norm_spread, 1)

            def turn(pe, source, ident, to):
                for k in range(KH):
                    last = pe.transpose(to[:, k * P:(k + 1) * P], source[:, k * P:(k + 1) * P], ident[:])
                return last

            def pe_dense(pe, step, c, more=False):
                if step == 1:
                    pe.wait_ge(sums_moved, c * 2 + 6)
                    turn(pe, pooled, identity, turned_ps).then_inc(turned, 1)
                if step == 2:
                    pe.wait_ge(turned_moved, c * 3 + 1)
                    if more:
                        pe.wait_ge(pool_scale_made, c + 3)
                    for k in range(KH):
                        last = pe.matmul(dense_ps[:], pooled_t[:, k, :], w_rec[:, k, :],
                                         start=(k == 0), stop=(k == KH - 1))
                    last.then_inc(dense_done, 1)
                    turn(pe, retrieved, identity, turned_ps).then_inc(turned, 1)
                if step == 3:
                    pe.wait_ge(turned_moved, c * 3 + 2)
                    pe.wait_ge(dense_moved, c * 2 + 1)
                    turn(pe, user_rep, identity, turned_ps).then_inc(turned, 1)
                if step == 4:
                    pe.wait_ge(gate_weights_in, 16)
                    pe.wait_ge(turned_moved, c * 3 + 3)
                    for k in range(2 * KH):
                        side = user_t if k < KH else retrieved_t
                        last = pe.matmul(dense_ps[:], side[:, k % KH, :], w_gate[:, k, :],
                                         start=(k == 0), stop=(k == 2 * KH - 1))
                    last.then_inc(dense_done, 1)
                if step == 7:
                    pe.wait_ge(low_half, c + 1)
                    for t in range(2):
                        last = turn(pe, halves[:, t, :], identity_h, turned_half[:, t * H:(t + 1) * H])
                    last.then_inc(turned, 1)

            def act_dense(act, step, c):
                if step == 1:
                    act.wait_ge(turned, c * 4 + 1)
                    act.activation(pooled_t[:].rearrange("p k u -> p (k u)"), turned_ps[:], ACT.Copy)\
                        .then_inc(turned_moved, 1)
                if step == 2:
                    act.wait_ge(turned, c * 4 + 2)
                    act.activation(retrieved_t[:].rearrange("p k u -> p (k u)"), turned_ps[:], ACT.Copy)\
                        .then_inc(turned_moved, 1)
                if step == 3:
                    act.wait_ge(turned, c * 4 + 3)
                    act.activation(user_t[:].rearrange("p k u -> p (k u)"), turned_ps[:], ACT.Copy)\
                        .then_inc(turned_moved, 1)
                if step == 5:
                    act.wait_ge(dense_moved, c * 2 + 2)
                    act.activation(gate[:], gate[:], ACT.Sigmoid).then_inc(gate_made, 1)
                if step == 6:
                    act.wait_ge(mixed, c + 1)
                    act.activation(halves[:, 0, :], mix[:], ACT.Copy, scale=fused_scale[:, 0:1])\
                        .then_inc(high_half, 1)
                if step == 7:
                    act.wait_ge(turned, c * 4 + 4)
                    act.wait_ge(fused_stored, c * 16 + 16)
                    act.activation(halves_t[:].rearrange("p k u -> p (k u)"), turned_half[:], ACT.Copy)\
                        .then_inc(halves_moved, 1)
                    act.wait_ge(halves_moved, c + 1)
                    act.dma_start(fused_parts[:, bass.ds(c * (2 * H), 2 * H)],
                                  halves_t[:].rearrange("p k u -> p (k u)")).then_inc(fused_stored, 16)

            def dve_dense(dve, step, c):
                if step == 2:
                    dve.wait_ge(dense_done, c * 2 + 1)
                    dve.tensor_tensor(user_rep[:], dense_ps[:], b_rec_all[:], ALU.add).then_inc(dense_moved, 1)
                if step == 4:
                    dve.wait_ge(dense_done, c * 2 + 2)
                    dve.tensor_tensor(gate[:], dense_ps[:], b_gate_all[:], ALU.add).then_inc(dense_moved, 1)
                if step == 5:
                    dve.tensor_tensor(mix[:], user_rep[:], retrieved[:], ALU.subtract)
                    dve.drain()
                    dve.wait_ge(gate_made, c + 1)
                    dve.tensor_tensor(mix[:], mix[:], gate[:], ALU.mult)
                    dve.drain()
                    dve.tensor_tensor(mix[:], mix[:], retrieved[:], ALU.add)
                    dve.drain()
                    dve.tensor_reduce(fused_peak[:], mix[:], AX.X, ALU.max, apply_absolute_value=True)
                    dve.drain()
                    scale_from_peak(dve, fused_peak[:], fused_expo[:], fused_scale[:], fused_unscale_1[:])
                    dve.tensor_copy(fused_unscale[:, bass.ds(c, 1)], fused_unscale_1[:])
                    dve.drain().then_inc(mixed, 1)
                if step == 6:
                    dve.wait_ge(high_half, c + 1)
                    dve.scalar_tensor_tensor(halves[:, 1, :], mix[:], fused_scale[:, 0:1], halves[:, 0, :],
                                             ALU.mult, ALU.subtract).then_inc(low_half, 1)

            def move_sums(act, c):
                act.wait_ge(block_pooled, c + 2)
                act.wait_ge(pool_scale_made, c + 1)
                act.activation(pooled[:], pooled_ps[:, bass.ds(c % 2 * 2, 1), :], ACT.Copy,
                               scale=pool_scale[:, bass.ds(c, 1)]).then_inc(sums_moved, 1)
                act.activation(retrieved[:], pooled_ps[:, bass.ds(c % 2 * 2 + 1, 1), :], ACT.Copy,
                               scale=ret_scale[:, 0:1]).then_inc(sums_moved, 1)

            @block1.tensor
            def _(pe):
                for s in ring_used + [first_used, block_pooled]:
                    pe.sem_inc(s, 1)

                def pool_chunk(b, chunk, parts, start, stop):
                    for t in range(2):
                        users = counts[:, bass.ds(b % 2, 1), bass.ds(chunk + t * NQ, 1), :]
                        for half in range(2):
                            last = pe.matmul(pooled_ps[:, bass.ds(b % 2 * 2 + t, 1), :], users, parts[:, half, :],
                                             start=start and half == 0, stop=stop and half == 1)
                    return last

                def pool_block(b, more, dense):
                    pe.wait_ge(pair_moved, b * PAIRS + (PAIRS + 2))
                    pe.wait_ge(sums_moved, b * 2 + 2)
                    if dense:
                        pe.wait_ge(first_in, b * 16)
                    else:
                        pe.wait_ge(edges_made, 1)
                    pool_chunk(b, 0, first_chunk, True, False).then_inc(first_used, 1)
                    with pe.Fori(0, STEPS) as i:
                        if more:
                            with pe.If(i == 0):
                                count_present(pe, b + 1)
                        if dense:
                            for step in (1, 2, 3, 4):
                                with pe.If(i == step):
                                    pe_dense(pe, step, b - 1, more)
                        for j in range(SLOTS):
                            if dense:
                                pe.wait_ge(ring_in[j], (b - 1) * (16 * STEPS) + i * 16 + 16)
                            else:
                                pe.wait_ge(parts_made, i * SLOTS + (j + 3))
                            for q in range(RC):
                                last = pool_chunk(b, i * (SLOTS * RC) + (j * RC + q + 1), ring[:, j, q],
                                                  False, False)
                            last.then_inc(ring_used[j], 1)
                            if more:
                                count_quad(pe, b * pl.quads + i * SLOTS + (pl.quads + j), j)
                    if dense:
                        pe.wait_ge(last_in, b * 16)
                    pool_chunk(b, NQ - 1, last_chunk, False, True).then_inc(block_pooled, 1)
                    if dense:
                        pe_dense(pe, 7, b - 1)
                    else:
                        pe.wait_ge(weights_in, 48)
                        pe.wait_ge(identity_made, 1)

                over_blocks(pe, pool_block)
                for step in (1, 2, 3, 4, 7):
                    pe_dense(pe, step, NB - 1)

            @block1.scalar
            def _(act):
                act.sem_inc(sums_moved, 4)
                act.sem_inc(fused_stored, 16)
                act.sem_inc(look_done, 1)

                def move_quad(b, i, j):
                    for h in range(2):
                        move_pair(act, b * PAIRS + i * (2 * SLOTS) + (PAIRS + 2 * j + h), h, (b + 1) % 2,
                                  i * (SLOTS * QUAD) + (j * QUAD + h * PAIR))

                def split_high(i, again):
                    for j in range(SLOTS):
                        act.wait_ge(chunks_in[j % 2], i * 32 + (j // 2 * 16 + 16))
                        if again:
                            act.wait_ge(ring_used[j], i + 1)
                            act.wait_ge(ring_stored[j], i * 16)
                        act.activation(ring[:, j, :, 0, :], stage32(j % 2), ACT.Copy, scale=scale[:, 0:1])\
                            .then_inc(high_made, 1)
                        if again or j > 0:
                            move_quad(0, i - (j == 0), (j - 1) % SLOTS)

                def split_block():
                    act.wait_ge(edges_in, 32)
                    for edge, to in zip(edges32, (first_chunk, last_chunk)):
                        act.activation(to[:, 0, :], edge, ACT.Copy, scale=scale[:, 0:1]).then_inc(edges_high, 1)
                    split_high(0, False)
                    with act.Fori(1, STEPS) as i:
                        split_high(i, True)
                    move_quad(0, STEPS - 1, SLOTS - 1)

                def move_block(b, more, dense):
                    if not dense:
                        return split_block()
                    move_sums(act, b - 1)
                    with act.Fori(0, STEPS) as i:
                        for j in range(SLOTS):
                            if more:
                                move_quad(b, i, j)
                            if j == 1:
                                for step in (1, 2, 3, 5, 6):
                                    with act.If(i == step):
                                        act_dense(act, step, b - 1)
                            if j == 2:
                                n = (b - 1) * STEPS + i
                                act.wait_ge(look_in, n * 16 + 16)
                                act.activation(look[:], look[:], ACT.Square, accum_out=proj_norm[:, bass.ds(n, 1)])\
                                    .then_inc(pieces_summed, 1)
                                act.drain().then_inc(look_done, 1)
                    act_dense(act, 7, b - 1)

                over_blocks(act, move_block)
                move_sums(act, NB - 1)
                for step in (1, 2, 3, 5, 6, 7):
                    act_dense(act, step, NB - 1)
                act.wait_ge(fused_stored, 16 * NB + 16)

            @block1.vector
            def _(dve):
                dve.sem_inc(parts_made, 2)
                dve.wait_ge(edges_high, 2)
                for edge, to in zip(edges32, (first_chunk, last_chunk)):
                    dve.scalar_tensor_tensor(to[:, 1, :], edge, scale[:, 0:1], to[:, 0, :], ALU.mult, ALU.subtract)
                dve.drain().then_inc(edges_made, 1)

                def ready_block(b, more, dense):
                    if more:
                        prepare_ids(dve, b + 1)
                    with dve.Fori(0, STEPS) as i:
                        for j in range(SLOTS):
                            if not dense:
                                dve.wait_ge(high_made, i * SLOTS + (j + 1))
                                dve.scalar_tensor_tensor(ring[:, j, :, 1, :], stage32(j % 2), scale[:, 0:1],
                                                         ring[:, j, :, 0, :], ALU.mult, ALU.subtract)\
                                    .then_inc(parts_made, 1)
                            if more:
                                make_hots(dve, b * pl.quads + i * SLOTS + (pl.quads + j), j,
                                          i * (SLOTS * QUAD) + j * QUAD)
                            if more and j == 1:
                                with dve.If(i == 1):
                                    scale_pool(dve, b + 1)
                            for step, at in DVE_DENSE_AT.items():
                                if dense and at[1] == j:
                                    with dve.If(i == at[0]):
                                        dve_dense(dve, step, b - 1)

                over_blocks(dve, ready_block)
                dve.wait_ge(pieces_summed, 2 * pl.prep_rounds + pl.looks)
                dve.tensor_reduce(norm[:, 1:2], proj_norm[:], AX.X, ALU.add).then_inc(norm_made, 1)
                for step in DVE_DENSE_AT:
                    dve_dense(dve, step, NB - 1)
                dve.wait_ge(norm_spread, 2)
                scale_from_squares(dve, norm_all[:, 1:2], expo[:, 1:2], scale[:, 1:2], unscale[:, 1:2])
                dve.tensor_scalar(out_scale[:], fused_unscale[:], unscale[:, 1:2], None, ALU.mult)
                dve.drain().then_inc(scale_made, 1)

        with ExitStack() as inner:
            W = pl.width
            GROUP = 4
            fused = sb("fused", [P, NB, 2, KH, P], F16, inner)
            strip = sb("strip", [P, KH, W], F32, inner)
            strip_parts = sb("strip_parts", [P, 2, 2, KH, W], F16, inner)
            bias = sb("bias", [P, 2, W], F32, inner)
            rows = sb("rows", [P, 2, GROUP, W], F32, inner)
            logit_ps = [count_ps[:, 0], count_ps[:, 1], pooled_ps[:, 0], pooled_ps[:, 1],
                        pooled_ps[:, 2], pooled_ps[:, 3], turned_ps, dense_ps]
            fused_in = sem("fused_in")
            strip_in = sem("strip_in")
            bias_in = sem("bias_in")
            strip_high = sem("strip_high")
            strip_split = sem("strip_split")
            logits_made = sem("logits_made")
            logits_moved = sem("logits_moved")
            rows_stored = [sem(f"rows_stored{s}") for s in range(2)]
            block2 = inner.enter_context(nc.Block())
            halves_n = NB // 8

            @block2.sync
            def _(sp):
                sp.dma_start(fused[:].rearrange("p b t k u -> p (b t k u)"), fused_parts).then_inc(fused_in, 16)
                for s in rows_stored:
                    sp.sem_inc(s, 16)

                def load(c):
                    cols = bass.ds(c * W, W)
                    sp.dma_start(strip[:], proj_t.rearrange("(k p) i -> p k i", p=P)[:, :, cols])\
                        .then_inc(strip_in, 16)
                    sp.dma_start(bias[:, bass.ds(c % 2, 1), :],
                                 proj_b.rearrange("(a n) -> a n", a=1)[:, cols].broadcast_to((P, W)))\
                        .then_inc(bias_in, 16)

                def store(c):
                    with sp.Fori(0, halves_n) as g:
                        for s in range(2):
                            sp.wait_ge(logits_moved, c * NB + g * 8 + (s * GROUP + GROUP + 8))
                            sp.dma_start(out.rearrange("(b p) i -> p b i", p=P)[
                                :, bass.ds(g * 8 + s * GROUP, GROUP), bass.ds(c * W, W)], rows[:, s])\
                                .then_inc(rows_stored[s], 16)

                load(0)
                with sp.Fori(0, pl.strips - 1) as c:
                    sp.wait_ge(strip_split, c + 1)
                    sp.wait_ge(logits_moved, c * NB + 8)
                    load(c + 1)
                    store(c)
                store(pl.strips - 1)
                for s in range(2):
                    sp.wait_ge(rows_stored[s], 16 * halves_n * pl.strips + 16)

            @block2.scalar
            def _(act):
                act.wait_ge(scale_made, 2)
                with act.Fori(0, pl.strips) as c:
                    act.wait_ge(strip_in, c * 16 + 16)
                    act.wait_ge(logits_made, c * NB + NB)
                    act.activation(strip_parts[:, bass.ds(c % 2, 1), 0], strip[:], ACT.Copy, scale=scale[:, 1:2])\
                        .then_inc(strip_high, 1)

            @block2.vector
            def _(dve):
                dve.sem_inc(logits_moved, 8)

                def split_low(c):
                    dve.wait_ge(bias_in, c * 16 + 16)
                    dve.wait_ge(strip_high, c + 1)
                    par = bass.ds(c % 2, 1)
                    dve.scalar_tensor_tensor(strip_parts[:, par, 1], strip[:], scale[:, 1:2],
                                             strip_parts[:, par, 0], ALU.mult, ALU.subtract)\
                        .then_inc(strip_split, 1)

                def move_logits(c, more):
                    if more:
                        split_low(c + 1)
                    with dve.Fori(0, halves_n) as g:
                        for s in range(2):
                            dve.wait_ge(rows_stored[s], c * (16 * halves_n) + g * 16 + 16)
                            for v in range(GROUP):
                                bank = s * GROUP + v
                                dve.wait_ge(logits_made, c * NB + g * 8 + (2 * NB + bank + 1))
                                dve.scalar_tensor_tensor(rows[:, s, v, :], logit_ps[bank][:, 0:W],
                                                         out_scale[:, bass.ds(g * 8 + bank, 1)],
                                                         bias[:, bass.ds(c % 2, 1), :], ALU.mult, ALU.add)\
                                    .then_inc(logits_moved, 1)

                split_low(0)
                with dve.Fori(0, pl.strips - 1) as c:
                    move_logits(c, True)
                move_logits(pl.strips - 1, False)

            @block2.tensor
            def _(pe):
                pe.sem_inc(logits_made, 2 * NB)
                pe.wait_ge(fused_in, 16)
                with pe.Fori(0, pl.strips) as c:
                    with pe.Fori(0, halves_n) as g:
                        pe.wait_ge(strip_split, c + 1)
                        for bank in range(8):
                            pe.wait_ge(logits_moved, c * NB + g * 8 + (bank + 1))
                            for k in range(KH):
                                for n, (f, w) in enumerate(((0, 0), (0, 1), (1, 0))):
                                    last = pe.matmul(logit_ps[bank][:, 0:W],
                                                     fused[:, bass.ds(g * 8 + bank, 1), f, k, :],
                                                     strip_parts[:, bass.ds(c % 2, 1), w, k, :],
                                                     start=(k == 0 and n == 0), stop=(k == KH - 1 and n == 2))
                            last.then_inc(logits_made, 1)


def scale_from_exponent(dve, expo, scale, unscale):
    dve.drain()
    dve.tensor_scalar(expo, expo, -1.0, float(2 * EXP_BIAS + F16_TOP + 1), ALU.mult, ALU.add)
    dve.drain()
    dve.tensor_scalar(expo, expo, float(2 * EXP_BIAS - 1), None, ALU.min)
    dve.drain()
    dve.tensor_scalar(scale.bitcast(I32), expo, 23, None, ALU.logical_shift_left)
    dve.drain()
    dve.tensor_scalar(expo, expo, -1.0, float(2 * EXP_BIAS), ALU.mult, ALU.add)
    dve.drain()
    dve.tensor_scalar(unscale.bitcast(I32), expo, 23, None, ALU.logical_shift_left)
    dve.drain()


def scale_from_peak(dve, peak, expo, scale, unscale):
    dve.tensor_scalar(expo, peak.bitcast(I32), 23, None, ALU.logical_shift_right)
    dve.drain()
    dve.tensor_scalar(expo, expo, 1.0, None, ALU.add)
    scale_from_exponent(dve, expo, scale, unscale)


def scale_from_squares(dve, squares, expo, scale, unscale):
    dve.tensor_scalar(expo, squares.bitcast(I32), 23, None, ALU.logical_shift_right)
    dve.drain()
    dve.tensor_scalar(expo, expo, float(EXP_BIAS + 2), None, ALU.add)
    dve.drain()
    dve.tensor_scalar(expo, expo, 1, None, ALU.logical_shift_right)
    scale_from_exponent(dve, expo, scale, unscale)


def kernel(r_sequence_ids, r_retrieved_indices, L0_rec_item_embeddings, L0_rec_W_rec, L0_rec_b_rec,
           L0_rec_gate_W, L0_rec_gate_b, L0_rec_proj_W, L0_rec_proj_b):
    import numpy as np
    import concourse.bacc as bacc
    from concourse.bass_utils import run_bass_kernel_spmd

    seq, ret = np.asarray(r_sequence_ids), np.asarray(r_retrieved_indices)
    table = np.asarray(L0_rec_item_embeddings)
    items, hidden = table.shape
    users, seq_len = seq.shape
    pl = Plan(seq_len, ret.shape[1], users, items, hidden)

    ids = np.zeros((P, 2, users), seq.dtype)
    ids[:, 0] = seq.T[:P]
    ids[:pl.low_seq, 1] = seq.T[P:]
    ids[pl.low_seq:pl.low_seq + pl.top_k, 1] = ret.T
    emb = np.zeros((pl.chunks * P, hidden), table.dtype)
    emb[:items] = table
    emb = np.ascontiguousarray(emb.reshape(pl.chunks, P, hidden).transpose(1, 0, 2)).reshape(P, -1)

    arrays = {
        "ids": ids, "emb": emb,
        "w_rec_t": np.ascontiguousarray(np.asarray(L0_rec_W_rec).T), "b_rec": np.asarray(L0_rec_b_rec),
        "w_gate_t": np.ascontiguousarray(np.asarray(L0_rec_gate_W).T), "b_gate": np.asarray(L0_rec_gate_b),
        "proj_t": np.ascontiguousarray(np.asarray(L0_rec_proj_W).T), "proj_b": np.asarray(L0_rec_proj_b),
    }
    nc = bacc.Bacc("TRN2", target_bir_lowering=False, num_devices=1)
    args = [nc.dram_tensor(name, a.shape, mybir.dt.from_np(a.dtype), kind="ExternalInput").ap()
            for name, a in arrays.items()]
    emb_parts = nc.dram_tensor("emb_parts", (P, pl.chunks * 2 * hidden), F16, kind="Internal").ap()
    fused_parts = nc.dram_tensor("fused_parts", (P, pl.blocks * 2 * hidden), F16, kind="Internal").ap()
    out = nc.dram_tensor("logits", (users, items), F32, kind="ExternalOutput").ap()
    pooling_program(nc, pl, *args, emb_parts, fused_parts, out)
    result = run_bass_kernel_spmd(nc, [arrays], core_ids=[0])
    return result.results[0]["logits"]
```

```python
from contextlib import ExitStack

import concourse.bass as bass
from concourse import mybir

F32 = mybir.dt.float32
F16 = mybir.dt.float16
I32 = mybir.dt.int32
ALU = mybir.AluOpType
ACT = mybir.ActivationFunctionType
AX = mybir.AxisListType

P = 128
G = 2 * P
STEPS = 8
SLOTS = 4
QUAD = 4
SUMS = 5
HALVES = 2 * STEPS
DVE_DENSE_AT = {1: (0, 2), 2: (3, 1), 4: (5, 2), 5: (6, 3), 6: (7, 2)}
ABSENT = 512.0
F16_TOP = 14
EXP_BIAS = 127


class Plan:

    def __init__(self, seq_len, top_k, users, items, hidden):
        self.seq_len, self.top_k = seq_len, top_k
        self.users, self.items, self.hidden = users, items, hidden
        self.blocks = users // P
        self.kh = hidden // P
        self.chunks = -(-items // P)
        self.low_seq = seq_len - P
        self.ring_chunks = (self.chunks - 2) // (STEPS * SLOTS)
        assert self.ring_chunks * STEPS * SLOTS + 2 == self.chunks
        self.prep_chunks = next(n for n in range(8, 0, -1) if self.chunks % (2 * n) == 0)
        self.prep_rounds = self.chunks // (2 * self.prep_chunks)
        self.width = next(n for n in range(512, 0, -1) if items % n == 0)
        self.strips = items // self.width
        self.groups = users // G
        self.quads = G // QUAD
        self.piece_quads = 4
        assert self.quads == 2 * STEPS * SLOTS and self.quads >= 2 * self.prep_rounds * self.piece_quads
        assert users % (8 * P) == 0 and hidden == 512
        self.gather_rounds = top_k // SUMS
        assert self.gather_rounds * SUMS == top_k and self.gather_rounds % 2 == 0
        self.copies = 32
        assert self.items + self.copies - 1 <= self.chunks * P
        self.looks = (self.groups - 1) * HALVES
        self.look_step = hidden // P * items // self.looks
        self.look_cols = hidden // P * items - self.look_step * (self.looks - 1)


def pooling_program(nc, pl, ids, ret_ids, emb, w_rec_t, b_rec, w_gate_t, b_gate, proj_t, proj_b, emb_parts, fused_parts, out):
    NB, NG, KH, NQ, H = pl.blocks, pl.groups, pl.kh, pl.chunks, pl.hidden
    RC = pl.ring_chunks
    K = pl.top_k
    ROW_U, CH_U, ROW_L, CH_L = 0, P, P + NQ, 2 * P + NQ
    HOT = 2 * P + 2 * NQ

    with ExitStack() as outer:
        def sem(name):
            return outer.enter_context(nc.semaphore(name))

        def sb(name, shape, dt, scope=outer):
            return scope.enter_context(nc.sbuf_tensor(name, shape, dt))

        counts = sb("counts", [P, 2, NQ, G], F16)
        hots = sb("hots", [P, SLOTS, QUAD, HOT], F16)
        columns = sb("columns", [P, P], F16)
        raw_ids = sb("raw_ids", [P, 2, G], I32)
        row_of = sb("row_of", [P, 2, G], F32)
        chunk_of = sb("chunk_of", [P, 2, G], F32)
        present = sb("present", [P, 2, G], F16)
        ones = sb("ones", [P, 1], F16)
        ret_rows = sb("ret_rows", [P, NB * K + SUMS], I32)
        rows_now = sb("rows_now", [P, 2, SUMS], I32)
        gathered = sb("gathered", [P, SUMS, H], F32)
        emb_norm = sb("emb_norm", [P, 2 * pl.prep_rounds], F32)
        proj_norm = sb("proj_norm", [P, pl.looks], F32)
        norm = sb("norm", [P, 2], F32)
        norm_all = sb("norm_all", [P, 2], F32)
        expo = sb("expo", [P, 2], I32)
        scale = sb("scale", [P, 2], F32)
        unscale = sb("unscale", [P, 2], F32)
        pool_scale = sb("pool_scale", [P, NB], F32)
        warm = sb("warm", [P, 1], F32)
        present_n = sb("present_n", [P, 2], F32)
        present_r = sb("present_r", [P, 2], F32)
        fused_unscale = sb("fused_unscale", [P, NB], F32)
        out_scale = sb("out_scale", [P, NB], F32)

        count_ps = outer.enter_context(nc.psum_tensor("count_ps", [P, 2, 512], F32))
        pooled_ps = outer.enter_context(nc.psum_tensor("pooled_ps", [P, 4, 512], F32))
        turned_ps = outer.enter_context(nc.psum_tensor("turned_ps", [P, 512], F32))
        dense_ps = outer.enter_context(nc.psum_tensor("dense_ps", [P, 512], F32))
        turned_half = turned_ps[:].bitcast(F16)
        present_ps = dense_ps[:, 0:2]

        ids_in = sem("ids_in")
        consts_made = sem("consts_made")
        stage_in = [sem(f"stage_in{s}") for s in range(2)]
        stage_free = [sem(f"stage_free{s}") for s in range(2)]
        pieces_summed = sem("pieces_summed")
        norm_made = sem("norm_made")
        norm_spread = sem("norm_spread")
        scale_made = sem("scale_made")
        ids_ready = sem("ids_ready")
        present_counted = sem("present_counted")
        pool_scale_made = sem("pool_scale_made")
        hots_made = sem("hots_made")
        quad_counted = sem("quad_counted")
        quad_moved = sem("quad_moved")
        ret_ids_in = sem("ret_ids_in")
        ret_rows_made = sem("ret_rows_made")
        gather_done = [sem(f"gather_done{a}") for a in range(SUMS)]
        rows_copied = sem("rows_copied")
        gathered_used = sem("gathered_used")

        def prepare_ids(dve, block):
            dve.drain()
            dve.wait_ge(ids_in, 16 * (block + 1))
            dve.tensor_scalar(chunk_of[:], raw_ids[:], -1.0, None, ALU.add)
            dve.tensor_scalar(row_of[:], raw_ids[:], 0.0, ABSENT, ALU.is_equal, ALU.mult)
            dve.wait_ge(present_counted, block + 1)
            dve.tensor_scalar(present[:], raw_ids[:], 0.0, None, ALU.not_equal)
            dve.drain()
            clamped = chunk_of[:].bitcast(I32)
            dve.tensor_scalar(clamped, chunk_of[:], 0.0, float(pl.items - 1), ALU.max, ALU.min)
            dve.drain()
            row_bits = raw_ids
            dve.tensor_scalar(row_bits[:], clamped, P - 1, None, ALU.bitwise_and)
            dve.tensor_scalar(clamped, clamped, 7, None, ALU.logical_shift_right)
            dve.drain()
            dve.tensor_tensor(row_of[:], row_bits[:], row_of[:], ALU.add)
            dve.tensor_copy(chunk_of[:], clamped)
            dve.drain().then_inc(ids_ready, 1)

        def gather_round(pool, block, r, turn):
            first = isinstance(r, int) and r == 0
            for a in range(SUMS):
                if not first:
                    pool.wait_ge(gather_done[a], block * (pl.gather_rounds * 16) + r * 16)
                pool.wait_ge(rows_copied, block * K + r * SUMS + (a + 1))
                pool.tensor_copy(rows_now[:, 1 - turn, a:a + 1],
                                 ret_rows[:, bass.ds(block * K + r * SUMS + (a + SUMS), 1)]).then_inc(rows_copied, 1)
                mode = {} if first else dict(compute_op=ALU.add)
                pool.indirect_dma_start(gathered[:, a, :], None, emb.rearrange("p (c h) -> (p c) h", h=H),
                                        bass.IndirectOffsetOnAxis(rows_now[:, turn, a:a + 1], 0), **mode)\
                    .then_inc(gather_done[a], 16)

        def gather_block(pool, block):
            gather_round(pool, block, 0, 0)
            gather_round(pool, block, 1, 1)
            with pool.Fori(1, pl.gather_rounds // 2) as r:
                for turn in range(2):
                    gather_round(pool, block, r * 2 + turn, turn)

        def count_present(pe, block):
            pe.wait_ge(ids_ready, block + 1)
            if not (isinstance(block, int) and block == 0):
                pe.wait_ge(pool_scale_made, block)
            for d in range(2):
                for part in range(2):
                    last = pe.matmul(present_ps[:, d:d + 1], present[:, part, d * P:(d + 1) * P], ones[:],
                                     start=(part == 0), stop=(part == 1))
            last.then_inc(present_counted, 1)

        def scale_pool(dve, block):
            dve.wait_ge(present_counted, block + 2)
            dve.tensor_scalar(present_n[:], present_ps, 1.0, None, ALU.max)
            dve.drain()
            dve.reciprocal(present_r[:], present_n[:])
            dve.drain()
            dve.tensor_scalar(pool_scale[:, bass.ds(block * 2, 2)], present_r[:], unscale[:, 0:1], None, ALU.mult)
            dve.drain().then_inc(pool_scale_made, 1)

        def make_hots(dve, quad, slot, first_user):
            dve.wait_ge(quad_counted, quad + 1)
            for v in range(QUAD):
                u = bass.ds(first_user + v, 1)
                for at, n, of, part in ((ROW_U, P, row_of, 0), (CH_U, NQ, chunk_of, 0),
                                        (ROW_L, P, row_of, 1), (CH_L, NQ, chunk_of, 1)):
                    last = dve.tensor_scalar(hots[:, slot, v, at:at + n], columns[:, 0:n], of[:, part, u],
                                             None, ALU.is_equal)
            last.then_inc(hots_made, 1)

        def count_quad(pe, quad, slot):
            pe.wait_ge(hots_made, quad + 1)
            pe.wait_ge(quad_moved, quad + 1)
            for v in range(QUAD):
                hot = hots[:, slot, v, :]
                to = count_ps[:, slot % 2, v * NQ:(v + 1) * NQ]
                pe.matmul(to, hot[:, ROW_L:ROW_L + P], hot[:, CH_L:CH_L + NQ], start=True, stop=False)
                last = pe.matmul(to, hot[:, ROW_U:ROW_U + P], hot[:, CH_U:CH_U + NQ], start=False, stop=True)
            last.then_inc(quad_counted, 1)

        def move_quad_counts(act, number, bank, parity, first_user):
            act.wait_ge(quad_counted, number + (SLOTS + 1))
            act.activation(counts[:, parity, :, bass.ds(first_user, QUAD)],
                           count_ps[:, bank, 0:QUAD * NQ].rearrange("p (u c) -> p c u", u=QUAD),
                           ACT.Copy).then_inc(quad_moved, 1)

        with ExitStack() as inner:
            PC = pl.prep_chunks
            E = pl.prep_rounds
            PQ = pl.piece_quads
            columns_i = sb("columns_i", [P, P], I32, inner)
            ids_by_user = sb("ids_by_user", [P, NB * K], I32, inner)
            wrapped = sb("wrapped", [P, NB * K], F32, inner)
            chunk_i = sb("chunk_i", [P, NB * K], I32, inner)
            last_row = sb("last_row", [P, 1], F32, inner)
            last_row_i = sb("last_row_i", [P, 1], I32, inner)
            stage = sb("stage", [P, 2, PC * H], F32, inner)
            block0 = inner.enter_context(nc.Block())

            @block0.sync
            def _(sp):
                sp.dma_start(ids_by_user[:], ret_ids).then_inc(ret_ids_in, 16)
                sp.dma_start(raw_ids[:], ids[:, :, 0:G]).then_inc(ids_in, 16)
                with sp.Fori(0, E) as r:
                    for s in range(2):
                        sp.wait_ge(stage_free[s], r + 1)
                        sp.dma_start(stage[:, s, :], emb[:, bass.ds((r * 2 + s) * PC * H, PC * H)])\
                            .then_inc(stage_in[s], 16)

            @block0.gpsimd
            def _(pool):
                pool.iota(columns_i[:], [[1, P]], base=0, channel_multiplier=0)
                pool.iota(last_row_i[:], [[0, 1]], base=0, channel_multiplier=1)
                pool.memset(ones[:], 1.0)
                pool.memset(ret_rows[:, NB * K:], 0)
                pool.drain().then_inc(consts_made, 1)
                pool.wait_ge(ret_rows_made, 1)
                pool.tensor_copy(rows_now[:, 0], ret_rows[:, 0:SUMS]).then_inc(rows_copied, SUMS)
                gather_block(pool, 0)
                pool.wait_ge(norm_made, 1)
                pool.partition_all_reduce(norm_all[:, 0:1], norm[:, 0:1], P, bass.bass_isa.ReduceOp.max)\
                    .then_inc(norm_spread, 1)

            @block0.vector
            def _(dve):
                dve.wait_ge(consts_made, 1)
                dve.tensor_copy(columns[:], columns_i[:])
                dve.tensor_scalar(last_row_i[:], last_row_i[:], pl.copies - 1, None, ALU.bitwise_and)
                dve.wait_ge(ret_ids_in, 16)
                dve.tensor_scalar(wrapped[:], ids_by_user[:], 0.0, float(pl.items), ALU.is_lt, ALU.mult)
                dve.drain()
                dve.tensor_scalar(last_row[:], last_row_i[:], float(pl.items - 1), None, ALU.add)
                dve.tensor_tensor(wrapped[:], wrapped[:], ids_by_user[:], ALU.add)
                dve.drain()
                dve.tensor_scalar(ids_by_user[:], wrapped[:], 0.0, last_row[:, 0:1], ALU.max, ALU.min)
                dve.drain()
                dve.tensor_scalar(ret_rows[:, 0:NB * K], ids_by_user[:], P - 1, None, ALU.bitwise_and)
                dve.tensor_scalar(chunk_i[:], ids_by_user[:], 7, None, ALU.logical_shift_right)
                dve.drain()
                dve.scalar_tensor_tensor(ret_rows[:, 0:NB * K], ret_rows[:, 0:NB * K], float(NQ), chunk_i[:], ALU.mult, ALU.add)
                dve.drain().then_inc(ret_rows_made, 1)
                prepare_ids(dve, 0)
                with dve.Fori(0, HALVES) as i:
                    for j in range(SLOTS):
                        make_hots(dve, i * SLOTS + j, j, i * (SLOTS * QUAD) + j * QUAD)
                dve.wait_ge(pieces_summed, 2 * E)
                dve.tensor_reduce(norm[:, 0:1], emb_norm[:], AX.X, ALU.add).then_inc(norm_made, 1)
                dve.wait_ge(norm_spread, 1)
                scale_from_squares(dve, norm_all[:, 0:1], expo[:, 0:1], scale[:, 0:1], unscale[:, 0:1])
                dve.drain().then_inc(scale_made, 1)
                scale_pool(dve, 0)

            @block0.scalar
            def _(act):
                act.wait_ge(consts_made, 1)
                act.activation(warm[:], ones[:], ACT.Sigmoid)
                act.sem_inc(quad_moved, 2)
                for s in range(2):
                    act.sem_inc(stage_free[s], 1)
                with act.Fori(0, E) as r:
                    for s in range(2):
                        act.wait_ge(stage_in[s], 16 * r + 16)
                        act.activation(stage[:, s, :], stage[:, s, :], ACT.Square,
                                       accum_out=emb_norm[:, bass.ds(r * 2 + s, 1)]).then_inc(pieces_summed, 1)
                        act.drain().then_inc(stage_free[s], 1)
                        for k in range(PQ):
                            move_quad_counts(act, r * (2 * PQ) + (PQ * s + k), k % 2, 0,
                                             r * (2 * PQ * QUAD) + (PQ * s + k) * QUAD)
                for m in range(2 * PQ * E, pl.quads):
                    move_quad_counts(act, m, m % 2, 0, m * QUAD)

            @block0.tensor
            def _(pe):
                pe.sem_inc(present_counted, 1)
                pe.sem_inc(quad_counted, SLOTS)
                pe.wait_ge(consts_made, 1)
                count_present(pe, 0)
                with pe.Fori(0, HALVES) as i:
                    for j in range(SLOTS):
                        count_quad(pe, i * SLOTS + j, j)

        with ExitStack() as inner:
            ring = sb("ring", [P, SLOTS, RC, 2, H], F16, inner)
            first_chunk = sb("first_chunk", [P, 2, H], F16, inner)
            last_chunk = sb("last_chunk", [P, 2, H], F16, inner)
            w_rec = sb("w_rec", [P, KH, H], F32, inner)
            w_gate = sb("w_gate", [P, 2 * KH, H], F32, inner)
            b_rec_all = sb("b_rec_all", [P, H], F32, inner)
            b_gate_all = sb("b_gate_all", [P, H], F32, inner)
            identity = sb("identity", [P, P], F32, inner)
            identity_h = sb("identity_h", [P, P], F16, inner)
            pooled = sb("pooled", [P, H], F32, inner)
            retrieved = sb("retrieved", [P, H], F32, inner)
            user_rep = sb("user_rep", [P, H], F32, inner)
            pooled_t = sb("pooled_t", [P, KH, P], F32, inner)
            user_t = pooled_t
            retrieved_t = sb("retrieved_t", [P, KH, P], F32, inner)
            gate = pooled
            mix = user_rep
            halves = sb("halves", [P, 2, H], F16, inner)
            halves_t = sb("halves_t", [P, 2 * KH, P], F16, inner)
            fused_peak = sb("fused_peak", [P, 1], F32, inner)
            fused_expo = sb("fused_expo", [P, 1], I32, inner)
            fused_scale = sb("fused_scale", [P, 1], F32, inner)
            fused_unscale_1 = sb("fused_unscale_1", [P, 1], F32, inner)
            look = sb("look", [P, pl.look_cols], F32, inner)
            def stage32(s):
                return w_gate[:, s * KH:s * KH + RC, :]

            edges32 = (w_gate[:, RC, :], w_gate[:, KH + RC, :])
            assert RC < KH

            weights_in = sem("weights_in")
            gate_weights_in = sem("gate_weights_in")
            edges_in = sem("edges_in")
            edges_high = sem("edges_high")
            edges_made = sem("edges_made")
            edges_stored = sem("edges_stored")
            high_made = sem("high_made")
            parts_made = sem("parts_made")
            chunks_in = [sem(f"chunks_in{s}") for s in range(2)]
            ring_stored = [sem(f"ring_stored{s}") for s in range(SLOTS)]
            look_in = sem("look_in")
            look_done = sem("look_done")
            identity_made = sem("identity_made")
            ring_in = [sem(f"ring_in{s}") for s in range(SLOTS)]
            ring_used = [sem(f"ring_used{s}") for s in range(SLOTS)]
            first_in = sem("first_in")
            first_used = sem("first_used")
            last_in = sem("last_in")
            block_pooled = sem("block_pooled")
            sums_moved = sem("sums_moved")
            retrieved_made = sem("retrieved_made")
            turned = sem("turned")
            turned_moved = sem("turned_moved")
            dense_done = sem("dense_done")
            dense_moved = sem("dense_moved")
            gate_made = sem("gate_made")
            mixed = sem("mixed")
            high_half = sem("high_half")
            low_half = sem("low_half")
            halves_moved = sem("halves_moved")
            fused_stored = sem("fused_stored")
            block1 = inner.enter_context(nc.Block())

            def over_blocks(eng, body):
                body(0, True, False)
                with eng.Fori(1, NG - 1) as b:
                    body(b, True, True)
                body(NG - 1, False, True)

            def dense_steps(eng, i, h, steps, run):
                for d in range(2):
                    for step, at in steps.items():
                        at += d * (HALVES // 2)
                        if at % 2 == h and at < HALVES:
                            with eng.If(i == at // 2):
                                run(step, d)

            @block1.sync
            def _(sp):
                parts = emb_parts.rearrange("p (c t h) -> p c t h", t=2, h=H)
                table = emb.rearrange("p (c h) -> p c h", h=H)
                def next_ids(b):
                    sp.wait_ge(ids_ready, b + 1)
                    sp.dma_start(raw_ids[:], ids[:, :, bass.ds(b * G + G, G)]).then_inc(ids_in, 16)

                def stream_table():
                    for to, chunk in zip(edges32, (0, NQ - 1)):
                        sp.dma_start(to, table[:, chunk]).then_inc(edges_in, 16)
                    next_ids(0)
                    with sp.Fori(0, STEPS) as i:
                        for j in range(SLOTS):
                            sp.wait_ge(parts_made, i * SLOTS + (j + 1))
                            sp.dma_start(stage32(j % 2), table[:, bass.ds(i * (SLOTS * RC) + (j * RC + 1), RC)])\
                                .then_inc(chunks_in[j % 2], 16)
                    sp.dma_start(w_rec[:], w_rec_t.rearrange("(k p) n -> p k n", p=P)).then_inc(weights_in, 16)
                    for to, of in ((b_rec_all, b_rec), (b_gate_all, b_gate)):
                        sp.dma_start(to[:], of.rearrange("(a n) -> a n", a=1).broadcast_to((P, H)))\
                            .then_inc(weights_in, 16)
                    sp.wait_ge(parts_made, STEPS * SLOTS + 2)
                    sp.wait_ge(edges_made, 1)
                    sp.dma_start(w_gate[:], w_gate_t.rearrange("(k p) n -> p k n", p=P)).then_inc(gate_weights_in, 16)
                    sp.wait_ge(edges_stored, 32)
                    for j in range(SLOTS):
                        sp.wait_ge(ring_stored[j], 16 * STEPS)

                def stream(b, more, later):
                    if not later:
                        return stream_table()
                    sp.wait_ge(first_used, b + 1)
                    sp.dma_start(first_chunk[:], parts[:, 0]).then_inc(first_in, 16)
                    if more:
                        next_ids(b)
                    with sp.Fori(0, STEPS) as i:
                        for j in range(SLOTS):
                            sp.wait_ge(ring_used[j], b * STEPS + i + 1)
                            sp.dma_start(ring[:, j], parts[:, bass.ds(i * (SLOTS * RC) + (j * RC + 1), RC)])\
                                .then_inc(ring_in[j], 16)
                    sp.wait_ge(block_pooled, b + 1)
                    sp.dma_start(last_chunk[:], parts[:, NQ - 1]).then_inc(last_in, 16)

                over_blocks(sp, stream)

            @block1.gpsimd
            def _(pool):
                pool.memset(identity[:], 1.0)
                pool.drain()
                pool.affine_select(out=identity[:], in_=identity[:], pattern=[[-1, P]], compare_op=ALU.is_equal,
                                   fill=0.0, base=0, channel_multiplier=1)
                pool.drain()
                pool.tensor_copy(identity_h[:], identity[:])
                pool.drain().then_inc(identity_made, 1)
                parts = emb_parts.rearrange("p (c t h) -> p c t h", t=2, h=H)
                pool.wait_ge(edges_made, 1)
                pool.dma_start(parts[:, 0], first_chunk[:]).then_inc(edges_stored, 16)
                pool.dma_start(parts[:, NQ - 1], last_chunk[:]).then_inc(edges_stored, 16)
                with pool.Fori(0, STEPS) as i:
                    for j in range(SLOTS):
                        pool.wait_ge(parts_made, i * SLOTS + (j + 3))
                        pool.dma_start(parts[:, bass.ds(i * (SLOTS * RC) + (j * RC + 1), RC)], ring[:, j])\
                            .then_inc(ring_stored[j], 16)
                with pool.Fori(1, NB) as b:
                    pool.wait_ge(gathered_used, b)
                    gather_block(pool, b)
                pool.wait_ge(norm_made, 2)
                pool.partition_all_reduce(norm_all[:, 1:2], norm[:, 1:2], P, bass.bass_isa.ReduceOp.max)\
                    .then_inc(norm_spread, 1)

            def turn(pe, source, ident, to):
                for k in range(KH):
                    last = pe.transpose(to[:, k * P:(k + 1) * P], source[:, k * P:(k + 1) * P], ident[:])
                return last

            def pe_dense(pe, step, c, d, next_group=None):
                if step == 1:
                    if d == 1:
                        pe.wait_ge(halves_moved, c)
                    pe.wait_ge(sums_moved, c + 5)
                    turn(pe, pooled, identity, turned_ps).then_inc(turned, 1)
                if step == 2:
                    pe.wait_ge(turned_moved, c * 3 + 1)
                    if next_group is not None:
                        pe.wait_ge(pool_scale_made, next_group + 1)
                    for k in range(KH):
                        last = pe.matmul(dense_ps[:], pooled_t[:, k, :], w_rec[:, k, :],
                                         start=(k == 0), stop=(k == KH - 1))
                    last.then_inc(dense_done, 1)
                    pe.wait_ge(retrieved_made, c + 1)
                    turn(pe, retrieved, identity, turned_ps).then_inc(turned, 1)
                if step == 3:
                    pe.wait_ge(turned_moved, c * 3 + 2)
                    pe.wait_ge(dense_moved, c * 2 + 1)
                    turn(pe, user_rep, identity, turned_ps).then_inc(turned, 1)
                if step == 4:
                    pe.wait_ge(gate_weights_in, 16)
                    pe.wait_ge(turned_moved, c * 3 + 3)
                    for k in range(2 * KH):
                        side = user_t if k < KH else retrieved_t
                        last = pe.matmul(dense_ps[:], side[:, k % KH, :], w_gate[:, k, :],
                                         start=(k == 0), stop=(k == 2 * KH - 1))
                    last.then_inc(dense_done, 1)
                if step == 7:
                    pe.wait_ge(low_half, c + 1)
                    for t in range(2):
                        last = turn(pe, halves[:, t, :], identity_h, turned_half[:, t * H:(t + 1) * H])
                    last.then_inc(turned, 1)

            def act_dense(act, step, c):
                if step == 1:
                    act.wait_ge(turned, c * 4 + 1)
                    act.activation(pooled_t[:].rearrange("p k u -> p (k u)"), turned_ps[:], ACT.Copy)\
                        .then_inc(turned_moved, 1)
                if step == 2:
                    act.wait_ge(turned, c * 4 + 2)
                    act.activation(retrieved_t[:].rearrange("p k u -> p (k u)"), turned_ps[:], ACT.Copy)\
                        .then_inc(turned_moved, 1)
                if step == 3:
                    act.wait_ge(turned, c * 4 + 3)
                    act.activation(user_t[:].rearrange("p k u -> p (k u)"), turned_ps[:], ACT.Copy)\
                        .then_inc(turned_moved, 1)
                if step == 5:
                    act.wait_ge(dense_moved, c * 2 + 2)
                    act.activation(gate[:], gate[:], ACT.Sigmoid).then_inc(gate_made, 1)
                if step == 6:
                    act.wait_ge(mixed, c + 1)
                    act.activation(halves[:, 0, :], mix[:], ACT.Copy, scale=fused_scale[:, 0:1])\
                        .then_inc(high_half, 1)
                if step == 7:
                    act.wait_ge(turned, c * 4 + 4)
                    act.wait_ge(fused_stored, c * 16 + 16)
                    act.activation(halves_t[:].rearrange("p k u -> p (k u)"), turned_half[:], ACT.Copy)\
                        .then_inc(halves_moved, 1)
                    act.wait_ge(halves_moved, c + 1)
                    act.dma_start(fused_parts[:, bass.ds(c * (2 * H), 2 * H)],
                                  halves_t[:].rearrange("p k u -> p (k u)")).then_inc(fused_stored, 16)

            def dve_dense(dve, step, c):
                if step == 1:
                    for a in range(SUMS):
                        dve.wait_ge(gather_done[a], c * (16 * pl.gather_rounds) + 16 * pl.gather_rounds)
                    dve.tensor_tensor(gathered[:, 0:2, :], gathered[:, 0:2, :], gathered[:, 2:4, :], ALU.add)
                    dve.drain()
                    dve.tensor_tensor(gathered[:, 0, :], gathered[:, 0, :], gathered[:, 1, :], ALU.add)
                    dve.drain()
                    dve.tensor_tensor(retrieved[:], gathered[:, 0, :], gathered[:, 4, :], ALU.add)\
                        .then_inc(gathered_used, 1)
                    dve.drain()
                    dve.tensor_scalar(retrieved[:], retrieved[:], 1.0 / K, None, ALU.mult).then_inc(retrieved_made, 1)
                if step == 2:
                    dve.wait_ge(dense_done, c * 2 + 1)
                    dve.tensor_tensor(user_rep[:], dense_ps[:], b_rec_all[:], ALU.add).then_inc(dense_moved, 1)
                if step == 4:
                    dve.wait_ge(dense_done, c * 2 + 2)
                    dve.tensor_tensor(gate[:], dense_ps[:], b_gate_all[:], ALU.add).then_inc(dense_moved, 1)
                if step == 5:
                    dve.tensor_tensor(mix[:], user_rep[:], retrieved[:], ALU.subtract)
                    dve.drain()
                    dve.wait_ge(gate_made, c + 1)
                    dve.tensor_tensor(mix[:], mix[:], gate[:], ALU.mult)
                    dve.drain()
                    dve.tensor_tensor(mix[:], mix[:], retrieved[:], ALU.add)
                    dve.drain()
                    dve.tensor_reduce(fused_peak[:], mix[:], AX.X, ALU.max, apply_absolute_value=True)
                    dve.drain()
                    scale_from_peak(dve, fused_peak[:], fused_expo[:], fused_scale[:], fused_unscale_1[:])
                    dve.tensor_copy(fused_unscale[:, bass.ds(c, 1)], fused_unscale_1[:])
                    dve.drain().then_inc(mixed, 1)
                if step == 6:
                    dve.wait_ge(high_half, c + 1)
                    dve.scalar_tensor_tensor(halves[:, 1, :], mix[:], fused_scale[:, 0:1], halves[:, 0, :],
                                             ALU.mult, ALU.subtract).then_inc(low_half, 1)

            def move_sums(act, g, d):
                act.wait_ge(block_pooled, g + 2)
                act.wait_ge(pool_scale_made, g + 1)
                act.activation(pooled[:], pooled_ps[:, bass.ds(g % 2 * 2 + d, 1), :], ACT.Copy,
                               scale=pool_scale[:, bass.ds(g * 2 + d, 1)]).then_inc(sums_moved, 1)

            @block1.tensor
            def _(pe):
                for s in ring_used + [first_used, block_pooled]:
                    pe.sem_inc(s, 1)

                def pool_chunk(b, chunk, parts, start, stop):
                    for d in range(2):
                        users = counts[:, bass.ds(b % 2, 1), bass.ds(chunk, 1), d * P:(d + 1) * P]
                        for half in range(2):
                            last = pe.matmul(pooled_ps[:, bass.ds(b % 2 * 2 + d, 1), :], users, parts[:, half, :],
                                             start=start and half == 0, stop=stop and half == 1)
                    return last

                def pool_block(b, more, dense):
                    pe.wait_ge(quad_moved, b * pl.quads + (pl.quads + 2))
                    pe.wait_ge(sums_moved, b * 2 + 2)
                    if dense:
                        pe.wait_ge(first_in, b * 16)
                    else:
                        pe.wait_ge(edges_made, 1)
                    pool_chunk(b, 0, first_chunk, True, False).then_inc(first_used, 1)
                    with pe.Fori(0, STEPS) as i:
                        if more:
                            with pe.If(i == 0):
                                count_present(pe, b + 1)
                        for j in range(SLOTS):
                            if dense and j % 2 == 0:
                                dense_steps(pe, i, j // 2, {1: 1, 2: 2, 3: 3, 4: 4, 7: 8}, lambda step, d:
                                            pe_dense(pe, step, (b - 1) * 2 + d, d, b + 1 if more and d == 0 else None))
                            if dense:
                                pe.wait_ge(ring_in[j], (b - 1) * (16 * STEPS) + i * 16 + 16)
                            else:
                                pe.wait_ge(parts_made, i * SLOTS + (j + 3))
                            for q in range(RC):
                                last = pool_chunk(b, i * (SLOTS * RC) + (j * RC + q + 1), ring[:, j, q],
                                                  False, False)
                            last.then_inc(ring_used[j], 1)
                            if more:
                                for q in (j * 2, j * 2 + 1):
                                    count_quad(pe, b * pl.quads + i * (2 * SLOTS) + (pl.quads + q), q % SLOTS)
                    if dense:
                        pe.wait_ge(last_in, b * 16)
                    pool_chunk(b, NQ - 1, last_chunk, False, True).then_inc(block_pooled, 1)
                    if dense:
                        pe_dense(pe, 7, (b - 1) * 2 + 1, 1)
                    else:
                        pe.wait_ge(weights_in, 48)
                        pe.wait_ge(identity_made, 1)

                over_blocks(pe, pool_block)
                for d in range(2):
                    for step in (1, 2, 3, 4, 7):
                        pe_dense(pe, step, NB - 2 + d, d)

            @block1.scalar
            def _(act):
                looked = proj_t.rearrange("(p k) i -> p (k i)", p=P)
                act.sem_inc(sums_moved, 4)
                act.sem_inc(fused_stored, 16)
                act.sem_inc(look_done, 1)

                def move_slot(b, i, j):
                    for q in (j * 2, j * 2 + 1):
                        move_quad_counts(act, b * pl.quads + i * (2 * SLOTS) + (pl.quads + q), q % 2, (b + 1) % 2,
                                         i * (2 * SLOTS * QUAD) + q * QUAD)

                def split_high(i, again):
                    for j in range(SLOTS):
                        act.wait_ge(chunks_in[j % 2], i * 32 + (j // 2 * 16 + 16))
                        if again:
                            act.wait_ge(ring_used[j], i + 1)
                            act.wait_ge(ring_stored[j], i * 16)
                        act.activation(ring[:, j, :, 0, :], stage32(j % 2), ACT.Copy, scale=scale[:, 0:1])\
                            .then_inc(high_made, 1)
                        if again or j > 0:
                            move_slot(0, i - (j == 0), (j - 1) % SLOTS)

                def split_block():
                    act.wait_ge(edges_in, 32)
                    for edge, to in zip(edges32, (first_chunk, last_chunk)):
                        act.activation(to[:, 0, :], edge, ACT.Copy, scale=scale[:, 0:1]).then_inc(edges_high, 1)
                    split_high(0, False)
                    with act.Fori(1, STEPS) as i:
                        split_high(i, True)
                    move_slot(0, STEPS - 1, SLOTS - 1)

                def move_block(b, more, dense):
                    if not dense:
                        return split_block()
                    move_sums(act, b - 1, 0)

                    def dense_step(step, d):
                        act_dense(act, step, (b - 1) * 2 + d)
                        if step == 7:
                            move_sums(act, b - 1, 1)

                    with act.Fori(0, STEPS) as i:
                        for j in range(SLOTS):
                            if j % 2 == 0:
                                n = (b - 1) * HALVES + i * 2 + j // 2
                                act.wait_ge(look_done, n + 1)
                                act.dma_start(look[:], looked[:, bass.ds(n * pl.look_step, pl.look_cols)])\
                                    .then_inc(look_in, 16)
                            if more:
                                move_slot(b, i, j)
                            if j % 2 == 0:
                                dense_steps(act, i, j // 2, {1: 1, 2: 2, 3: 3, 5: 5, 6: 6, 7: 8}, dense_step)
                            if j % 2 == 1:
                                n = (b - 1) * HALVES + i * 2 + j // 2
                                act.wait_ge(look_in, n * 16 + 16)
                                act.activation(look[:], look[:], ACT.Square, accum_out=proj_norm[:, bass.ds(n, 1)])\
                                    .then_inc(pieces_summed, 1)
                                act.drain().then_inc(look_done, 1)
                    act_dense(act, 7, (b - 1) * 2 + 1)

                over_blocks(act, move_block)
                for d in range(2):
                    move_sums(act, NG - 1, d)
                    for step in (1, 2, 3, 5, 6, 7):
                        act_dense(act, step, NB - 2 + d)
                act.wait_ge(fused_stored, 16 * NB + 16)

            @block1.vector
            def _(dve):
                dve.sem_inc(parts_made, 2)
                dve.wait_ge(edges_high, 2)
                for edge, to in zip(edges32, (first_chunk, last_chunk)):
                    dve.scalar_tensor_tensor(to[:, 1, :], edge, scale[:, 0:1], to[:, 0, :], ALU.mult, ALU.subtract)
                dve.drain().then_inc(edges_made, 1)

                def ready_block(b, more, dense):
                    if more:
                        prepare_ids(dve, b + 1)
                    with dve.Fori(0, STEPS) as i:
                        for j in range(SLOTS):
                            if not dense:
                                dve.wait_ge(high_made, i * SLOTS + (j + 1))
                                dve.scalar_tensor_tensor(ring[:, j, :, 1, :], stage32(j % 2), scale[:, 0:1],
                                                         ring[:, j, :, 0, :], ALU.mult, ALU.subtract)\
                                    .then_inc(parts_made, 1)
                            for q in (j * 2, j * 2 + 1):
                                if more:
                                    make_hots(dve, b * pl.quads + i * (2 * SLOTS) + (pl.quads + q), q % SLOTS,
                                              i * (2 * SLOTS * QUAD) + q * QUAD)
                                if more and q == SLOTS + 1:
                                    with dve.If(i == 0):
                                        scale_pool(dve, b + 1)
                                if dense:
                                    due = {step: at[0] for step, at in DVE_DENSE_AT.items() if at[1] == q % SLOTS}
                                    dense_steps(dve, i, q // SLOTS, due, lambda step, d:
                                                dve_dense(dve, step, (b - 1) * 2 + d))

                over_blocks(dve, ready_block)
                dve.wait_ge(pieces_summed, 2 * pl.prep_rounds + pl.looks)
                dve.tensor_reduce(norm[:, 1:2], proj_norm[:], AX.X, ALU.add).then_inc(norm_made, 1)
                for d in range(2):
                    for step in DVE_DENSE_AT:
                        dve_dense(dve, step, NB - 2 + d)
                dve.wait_ge(norm_spread, 2)
                scale_from_squares(dve, norm_all[:, 1:2], expo[:, 1:2], scale[:, 1:2], unscale[:, 1:2])
                dve.tensor_scalar(out_scale[:], fused_unscale[:], unscale[:, 1:2], None, ALU.mult)
                dve.drain().then_inc(scale_made, 1)

        with ExitStack() as inner:
            W = pl.width
            GROUP = 4
            fused = counts[:].rearrange("p a c u -> p (a c u)")[:, 0:NB * 2 * KH * P]\
                .rearrange("p (b t k u) -> p b t k u", t=2, k=KH, u=P)
            strip = sb("strip", [P, KH, W], F32, inner)
            strip_parts = sb("strip_parts", [P, 2, 2, KH, W], F16, inner)
            bias = sb("bias", [P, 2, W], F32, inner)
            rows = sb("rows", [P, 2, GROUP, W], F32, inner)
            logit_ps = [count_ps[:, 0], count_ps[:, 1], pooled_ps[:, 0], pooled_ps[:, 1],
                        pooled_ps[:, 2], pooled_ps[:, 3], turned_ps, dense_ps]
            fused_in = sem("fused_in")
            strip_in = sem("strip_in")
            bias_in = sem("bias_in")
            strip_high = sem("strip_high")
            strip_split = sem("strip_split")
            logits_made = sem("logits_made")
            logits_moved = sem("logits_moved")
            rows_stored = [sem(f"rows_stored{s}") for s in range(2)]
            block2 = inner.enter_context(nc.Block())
            halves_n = NB // 8

            @block2.sync
            def _(sp):
                sp.dma_start(fused.rearrange("p b t k u -> p (b t k u)"), fused_parts).then_inc(fused_in, 16)
                for s in rows_stored:
                    sp.sem_inc(s, 16)

                def load(c):
                    cols = bass.ds(c * W, W)
                    sp.dma_start(strip[:], proj_t.rearrange("(k p) i -> p k i", p=P)[:, :, cols])\
                        .then_inc(strip_in, 16)
                    sp.dma_start(bias[:, bass.ds(c % 2, 1), :],
                                 proj_b.rearrange("(a n) -> a n", a=1)[:, cols].broadcast_to((P, W)))\
                        .then_inc(bias_in, 16)

                def store(c):
                    with sp.Fori(0, halves_n) as g:
                        for s in range(2):
                            sp.wait_ge(logits_moved, c * NB + g * 8 + (s * GROUP + GROUP + 8))
                            sp.dma_start(out.rearrange("(b p) i -> p b i", p=P)[
                                :, bass.ds(g * 8 + s * GROUP, GROUP), bass.ds(c * W, W)], rows[:, s])\
                                .then_inc(rows_stored[s], 16)

                load(0)
                with sp.Fori(0, pl.strips - 1) as c:
                    sp.wait_ge(strip_split, c + 1)
                    sp.wait_ge(logits_moved, c * NB + 8)
                    load(c + 1)
                    store(c)
                store(pl.strips - 1)
                for s in range(2):
                    sp.wait_ge(rows_stored[s], 16 * halves_n * pl.strips + 16)

            @block2.scalar
            def _(act):
                act.wait_ge(scale_made, 2)
                with act.Fori(0, pl.strips) as c:
                    act.wait_ge(strip_in, c * 16 + 16)
                    act.wait_ge(logits_made, c * NB + NB)
                    act.activation(strip_parts[:, bass.ds(c % 2, 1), 0], strip[:], ACT.Copy, scale=scale[:, 1:2])\
                        .then_inc(strip_high, 1)

            @block2.vector
            def _(dve):
                dve.sem_inc(logits_moved, 8)

                def split_low(c):
                    dve.wait_ge(bias_in, c * 16 + 16)
                    dve.wait_ge(strip_high, c + 1)
                    par = bass.ds(c % 2, 1)
                    dve.scalar_tensor_tensor(strip_parts[:, par, 1], strip[:], scale[:, 1:2],
                                             strip_parts[:, par, 0], ALU.mult, ALU.subtract)\
                        .then_inc(strip_split, 1)

                def move_logits(c, more):
                    if more:
                        split_low(c + 1)
                    with dve.Fori(0, halves_n) as g:
                        for s in range(2):
                            dve.wait_ge(rows_stored[s], c * (16 * halves_n) + g * 16 + 16)
                            for v in range(GROUP):
                                bank = s * GROUP + v
                                dve.wait_ge(logits_made, c * NB + g * 8 + (2 * NB + bank + 1))
                                dve.scalar_tensor_tensor(rows[:, s, v, :], logit_ps[bank][:, 0:W],
                                                         out_scale[:, bass.ds(g * 8 + bank, 1)],
                                                         bias[:, bass.ds(c % 2, 1), :], ALU.mult, ALU.add)\
                                    .then_inc(logits_moved, 1)

                split_low(0)
                with dve.Fori(0, pl.strips - 1) as c:
                    move_logits(c, True)
                move_logits(pl.strips - 1, False)

            @block2.tensor
            def _(pe):
                pe.sem_inc(logits_made, 2 * NB)
                pe.wait_ge(fused_in, 16)
                with pe.Fori(0, pl.strips) as c:
                    with pe.Fori(0, halves_n) as g:
                        pe.wait_ge(strip_split, c + 1)
                        for bank in range(8):
                            pe.wait_ge(logits_moved, c * NB + g * 8 + (bank + 1))
                            for k in range(KH):
                                for n, (f, w) in enumerate(((0, 0), (0, 1), (1, 0))):
                                    last = pe.matmul(logit_ps[bank][:, 0:W],
                                                     fused[:, bass.ds(g * 8 + bank, 1), f, k, :],
                                                     strip_parts[:, bass.ds(c % 2, 1), w, k, :],
                                                     start=(k == 0 and n == 0), stop=(k == KH - 1 and n == 2))
                            last.then_inc(logits_made, 1)


def scale_from_exponent(dve, expo, scale, unscale):
    dve.drain()
    dve.tensor_scalar(expo, expo, -1.0, float(2 * EXP_BIAS + F16_TOP + 1), ALU.mult, ALU.add)
    dve.drain()
    dve.tensor_scalar(expo, expo, float(2 * EXP_BIAS - 1), None, ALU.min)
    dve.drain()
    dve.tensor_scalar(scale.bitcast(I32), expo, 23, None, ALU.logical_shift_left)
    dve.drain()
    dve.tensor_scalar(expo, expo, -1.0, float(2 * EXP_BIAS), ALU.mult, ALU.add)
    dve.drain()
    dve.tensor_scalar(unscale.bitcast(I32), expo, 23, None, ALU.logical_shift_left)
    dve.drain()


def scale_from_peak(dve, peak, expo, scale, unscale):
    dve.tensor_scalar(expo, peak.bitcast(I32), 23, None, ALU.logical_shift_right)
    dve.drain()
    dve.tensor_scalar(expo, expo, 1.0, None, ALU.add)
    scale_from_exponent(dve, expo, scale, unscale)


def scale_from_squares(dve, squares, expo, scale, unscale):
    dve.tensor_scalar(expo, squares.bitcast(I32), 23, None, ALU.logical_shift_right)
    dve.drain()
    dve.tensor_scalar(expo, expo, float(EXP_BIAS + 2), None, ALU.add)
    dve.drain()
    dve.tensor_scalar(expo, expo, 1, None, ALU.logical_shift_right)
    scale_from_exponent(dve, expo, scale, unscale)


def kernel(r_sequence_ids, r_retrieved_indices, L0_rec_item_embeddings, L0_rec_W_rec, L0_rec_b_rec,
           L0_rec_gate_W, L0_rec_gate_b, L0_rec_proj_W, L0_rec_proj_b):
    import numpy as np
    import concourse.bacc as bacc
    from concourse.bass_utils import run_bass_kernel_spmd

    seq, ret = np.asarray(r_sequence_ids), np.asarray(r_retrieved_indices)
    table = np.asarray(L0_rec_item_embeddings)
    items, hidden = table.shape
    users, seq_len = seq.shape
    pl = Plan(seq_len, ret.shape[1], users, items, hidden)

    ids = np.zeros((P, 2, users), seq.dtype)
    ids[:, 0] = seq.T[:P]
    ids[:pl.low_seq, 1] = seq.T[P:]
    ret_ids = np.ascontiguousarray(ret.reshape(pl.blocks, P, -1).transpose(1, 0, 2)).reshape(P, -1)
    emb = np.empty((pl.chunks * P, hidden), table.dtype)
    emb[:items] = table
    emb[items:] = table[-1]
    emb = np.ascontiguousarray(emb.reshape(pl.chunks, P, hidden).transpose(1, 0, 2)).reshape(P, -1)

    arrays = {
        "ids": ids, "ret_ids": ret_ids, "emb": emb,
        "w_rec_t": np.ascontiguousarray(np.asarray(L0_rec_W_rec).T), "b_rec": np.asarray(L0_rec_b_rec),
        "w_gate_t": np.ascontiguousarray(np.asarray(L0_rec_gate_W).T), "b_gate": np.asarray(L0_rec_gate_b),
        "proj_t": np.ascontiguousarray(np.asarray(L0_rec_proj_W).T), "proj_b": np.asarray(L0_rec_proj_b),
    }
    nc = bacc.Bacc("TRN2", target_bir_lowering=False, num_devices=1)
    args = [nc.dram_tensor(name, a.shape, mybir.dt.from_np(a.dtype), kind="ExternalInput").ap()
            for name, a in arrays.items()]
    emb_parts = nc.dram_tensor("emb_parts", (P, pl.chunks * 2 * hidden), F16, kind="Internal").ap()
    fused_parts = nc.dram_tensor("fused_parts", (P, pl.blocks * 2 * hidden), F16, kind="Internal").ap()
    out = nc.dram_tensor("logits", (users, items), F32, kind="ExternalOutput").ap()
    pooling_program(nc, pl, *args, emb_parts, fused_parts, out)
    result = run_bass_kernel_spmd(nc, [arrays], core_ids=[0])
    return result.results[0]["logits"]
```
